# Optimizing a Trainium2 kernel written in Bass

```python
import numpy as np
import jax
import jax.numpy as jnp

def _softmax(x, axis=-1):
    return jax.nn.softmax(x, axis=axis)

def _gelu(x):
    return jax.nn.gelu(x, approximate=True)

def _silu(x):
    return jax.nn.silu(x)

def _sigmoid(x):
    return jax.nn.sigmoid(x)

def _layernorm(x, axis=-1, eps=1e-05):
    m = jnp.mean(x, axis=axis, keepdims=True)
    v = jnp.var(x, axis=axis, keepdims=True)
    return (x - m) / jnp.sqrt(v + eps)

def _scatter_add(tgt, idx, src, axis=0):
    return tgt.at[idx].add(src)

def _segment_sum(src, seg, n):
    return jax.ops.segment_sum(src, seg, n)
kernel_name = 'mk_adj_resnorm_d4_adj_r2_54c56e'

def setup_inputs(seed: int=0):
    np.random.seed(seed)
    _w = jnp.asarray

    def _rec_inputs():
        import jax
        import jax.numpy as jnp
        _gk = jax.random.key(seed)
        x = -0.003407 + 1.001 * jax.random.normal(jax.random.fold_in(_gk, 1), (64, 128, 128), jnp.float32)
        _w = (1.0 + jnp.arange(128, dtype=jnp.float32)) ** (-0.5)
        _w = _w / _w.mean()
        _pij = jnp.clip(0.015625 * _w[:, None] * _w[None, :], 0.0, 1.0)
        _a = jax.random.uniform(jax.random.fold_in(_gk, 2), (64, 128, 128)) < _pij
        _a = jnp.logical_or(_a, jnp.swapaxes(_a, -1, -2))
        _a = jnp.logical_or(_a, jnp.eye(128, dtype=bool))
        _af = _a.astype(jnp.float32)
        _af = _af * jax.random.uniform(jax.random.fold_in(_gk, 3), (64, 128, 128), jnp.float32, 0.05, 1)
        adj = _af
        _nm = jnp.ones((64, 128), dtype=bool)
        nodemask = _nm
        return (x, adj, nodemask)
    x, adj, nodemask = _rec_inputs()

    def _L0_gnn_setup():
        import jax, jax.numpy as jnp
        import numpy as np
        B, S, H, HID = (1, 512, 128, 128)
        LN_EPS = 1e-05

        def _layernorm(y, gamma, beta):
            mu = jnp.mean(y, axis=-1, keepdims=True)
            var = jnp.mean(jnp.square(y - mu), axis=-1, keepdims=True)
            return (y - mu) * jax.lax.rsqrt(var + LN_EPS) * gamma + beta
        key = jax.random.key(seed)
        ks = jax.random.split(key, 8)
        x = jax.random.normal(ks[0], (B, S, H), dtype=jnp.float32)
        adj = jax.random.uniform(ks[1], (B, S, S), dtype=jnp.float32)
        W1 = jax.random.normal(ks[2], (2 * H, HID), dtype=jnp.float32) / np.sqrt(2 * H)
        b1 = jnp.zeros((HID,), dtype=jnp.float32)
        W2 = jax.random.normal(ks[3], (HID, HID), dtype=jnp.float32) / np.sqrt(HID)
        b2 = jnp.zeros((HID,), dtype=jnp.float32)
        gamma = jnp.ones((HID,), dtype=jnp.float32)
        beta = jnp.zeros((HID,), dtype=jnp.float32)
        return {'x': x, 'adj': adj, 'W1': W1, 'b1': b1, 'W2': W2, 'b2': b2, 'gamma': gamma, 'beta': beta}
    _L0_gnn_all = _L0_gnn_setup()
    _L0_gnn_in = {k: v for k, v in _L0_gnn_all.items() if k in ('W1', 'b1', 'W2', 'b2', 'gamma', 'beta')}
    del _L0_gnn_all

    def _L1_gnn_setup():
        import jax, jax.numpy as jnp
        import numpy as np
        B, N, D_IN, D_HID = (4, 2048, 128, 128)
        key = jax.random.key(seed)
        k1, k2, k3, k4 = jax.random.split(key, 4)
        x = jax.random.normal(k1, (B, N, D_IN), dtype=jnp.float32)
        adj = jax.random.uniform(k2, (B, N, N), dtype=jnp.float32)
        W = jax.random.normal(k3, (D_HID, D_IN), dtype=jnp.float32) * np.sqrt(2.0 / D_IN)
        bound = 1.0 / np.sqrt(D_IN)
        b = jax.random.uniform(k4, (D_HID,), dtype=jnp.float32, minval=-bound, maxval=bound)
        return {'x': x, 'adj': adj, 'W': W, 'b': b}
    _L1_gnn_all = _L1_gnn_setup()
    _L1_gnn_in = {k: v for k, v in _L1_gnn_all.items() if k in ('W', 'b')}
    del _L1_gnn_all

    def _L2_gnn_setup():
        import jax, jax.numpy as jnp
        import numpy as np
        B, N, F, H = (16, 512, 128, 128)
        key = jax.random.key(seed)
        k1, k2, k3, k4, k5 = jax.random.split(key, 5)
        x = jax.random.normal(k1, (B, N, F), dtype=jnp.float32)
        adjacency = (jax.random.uniform(k2, (B, N, N)) < 0.05).astype(jnp.float32)
        node_mask = jax.random.uniform(k3, (B, N)) < 0.9
        W1 = jax.random.normal(k4, (F, H), dtype=jnp.float32) / np.sqrt(F)
        b1 = jnp.zeros((H,), dtype=jnp.float32)
        W2 = jax.random.normal(k5, (H, F), dtype=jnp.float32) / np.sqrt(H)
        b2 = jnp.zeros((F,), dtype=jnp.float32)
        eps = jnp.zeros((1,), dtype=jnp.float32)
        return {'x': x, 'adjacency': adjacency, 'node_mask': node_mask, 'W1': W1, 'b1': b1, 'W2': W2, 'b2': b2, 'eps': eps}
    _L2_gnn_all = _L2_gnn_setup()
    _L2_gnn_in = {k: v for k, v in _L2_gnn_all.items() if k in ('W1', 'b1', 'W2', 'b2', 'eps')}
    del _L2_gnn_all

    def _L3_gnn_setup():
        import jax, jax.numpy as jnp
        import numpy as np
        B, N, D, L = (16, 1024, 128, 3)
        LN_EPS = 1e-05

        def _layer_norm(z, gamma, beta):
            mu = jnp.mean(z, axis=-1, keepdims=True)
            var = jnp.mean(jnp.square(z - mu), axis=-1, keepdims=True)
            return (z - mu) * jax.lax.rsqrt(var + LN_EPS) * gamma + beta
        key = jax.random.key(seed)
        k_x, k_a, k_w = jax.random.split(key, 3)
        X = jax.random.normal(k_x, (B, N, D), dtype=jnp.float32)
        adj_mat = jax.random.uniform(k_a, (B, N, N), dtype=jnp.float32)
        limit = np.sqrt(6.0 / (D + D))
        Ws = jax.random.uniform(k_w, (L, D, D), dtype=jnp.float32, minval=-limit, maxval=limit)
        bs = jnp.zeros((L, D), dtype=jnp.float32)
        gammas = jnp.ones((L, D), dtype=jnp.float32)
        betas = jnp.zeros((L, D), dtype=jnp.float32)
        return {'X': X, 'adj_mat': adj_mat, 'Ws': Ws, 'bs': bs, 'gammas': gammas, 'betas': betas}
    _L3_gnn_all = _L3_gnn_setup()
    _L3_gnn_in = {k: v for k, v in _L3_gnn_all.items() if k in ('Ws', 'bs', 'gammas', 'betas')}
    del _L3_gnn_all
    return {'x': x, 'adj': adj, 'nodemask': nodemask, 'L0_gnn_W1': _L0_gnn_in['W1'], 'L0_gnn_b1': _L0_gnn_in['b1'], 'L0_gnn_W2': _L0_gnn_in['W2'], 'L0_gnn_b2': _L0_gnn_in['b2'], 'L0_gnn_gamma': _L0_gnn_in['gamma'], 'L0_gnn_beta': _L0_gnn_in['beta'], 'L1_gnn_W': _L1_gnn_in['W'], 'L1_gnn_b': _L1_gnn_in['b'], 'L2_gnn_W1': _L2_gnn_in['W1'], 'L2_gnn_b1': _L2_gnn_in['b1'], 'L2_gnn_W2': _L2_gnn_in['W2'], 'L2_gnn_b2': _L2_gnn_in['b2'], 'L2_gnn_eps': _L2_gnn_in['eps'], 'L3_gnn_Ws': _L3_gnn_in['Ws'], 'L3_gnn_bs': _L3_gnn_in['bs'], 'L3_gnn_gammas': _L3_gnn_in['gammas'], 'L3_gnn_betas': _L3_gnn_in['betas']}

def reference(x, adj, nodemask, L0_gnn_W1, L0_gnn_b1, L0_gnn_W2, L0_gnn_b2, L0_gnn_gamma, L0_gnn_beta, L1_gnn_W, L1_gnn_b, L2_gnn_W1, L2_gnn_b1, L2_gnn_W2, L2_gnn_b2, L2_gnn_eps, L3_gnn_Ws, L3_gnn_bs, L3_gnn_gammas, L3_gnn_betas):
    import jax
    import jax.numpy as jnp

    def _L0_gnn_ref(x, adj, W1, b1, W2, b2, gamma, beta):
        import jax, jax.numpy as jnp
        import numpy as np
        B, S, H, HID = (1, 512, 128, 128)
        LN_EPS = 1e-05

        def _layernorm(y, gamma, beta):
            mu = jnp.mean(y, axis=-1, keepdims=True)
            var = jnp.mean(jnp.square(y - mu), axis=-1, keepdims=True)
            return (y - mu) * jax.lax.rsqrt(var + LN_EPS) * gamma + beta
        hi = jnp.einsum('bsh,hk->bsk', x, W1[:H])
        hj = jnp.einsum('bsh,hk->bsk', x, W1[H:])
        h = jax.nn.relu(hi[:, :, None, :] + hj[:, None, :, :] + b1)
        y = jnp.einsum('bijk,kl->bijl', h, W2) + b2
        y = _layernorm(y, gamma, beta)
        out = jnp.einsum('bij,bijh->bih', adj, y)
        return out

    def _L1_gnn_ref(x, adj, W, b):
        import jax, jax.numpy as jnp
        import numpy as np
        B, N, D_IN, D_HID = (4, 2048, 128, 128)
        row_sum = jnp.sum(adj, axis=-1)
        d_inv_sqrt = jnp.where(row_sum > 0, row_sum ** (-0.5), 0.0)
        adj_norm = adj * d_inv_sqrt[..., :, None] * d_inv_sqrt[..., None, :]
        h = jnp.matmul(adj_norm, x)
        out = jax.nn.relu(jnp.einsum('bnd,hd->bnh', h, W) + b)
        return out

    def _L2_gnn_ref(x, adjacency, node_mask, W1, b1, W2, b2, eps):
        import jax, jax.numpy as jnp
        import numpy as np
        B, N, F, H = (16, 512, 128, 128)
        x_agg = jnp.einsum('bnf,bnm->bmf', x, adjacency)
        h = (1.0 + eps) * x + x_agg
        y = jnp.maximum(h @ W1 + b1, 0.0) @ W2 + b2
        return jnp.where(node_mask[..., None], y, jnp.zeros((), dtype=y.dtype))

    def _L3_gnn_ref(X, adj_mat, Ws, bs, gammas, betas):
        import jax, jax.numpy as jnp
        import numpy as np
        B, N, D, L = (16, 1024, 128, 3)
        LN_EPS = 1e-05

        def _layer_norm(z, gamma, beta):
            mu = jnp.mean(z, axis=-1, keepdims=True)
            var = jnp.mean(jnp.square(z - mu), axis=-1, keepdims=True)
            return (z - mu) * jax.lax.rsqrt(var + LN_EPS) * gamma + beta
        h = X
        for i in range(L):
            res = h
            hw = jnp.einsum('bnd,de->bne', h, Ws[i])
            agg = jnp.einsum('bij,bie->bje', adj_mat, hw)
            conv = agg + bs[i]
            h = jax.nn.relu(_layer_norm(conv + res, gammas[i], betas[i]))
        return h
    x = _layernorm(x + _L0_gnn_ref(x, adj, L0_gnn_W1, L0_gnn_b1, L0_gnn_W2, L0_gnn_b2, L0_gnn_gamma, L0_gnn_beta), axis=-1)
    x = _layernorm(x + _L1_gnn_ref(x, adj, L1_gnn_W, L1_gnn_b), axis=-1)
    x = _layernorm(x + _L2_gnn_ref(x, adj, nodemask, L2_gnn_W1, L2_gnn_b1, L2_gnn_W2, L2_gnn_b2, L2_gnn_eps), axis=-1)
    x = _layernorm(x + _L3_gnn_ref(x, adj, L3_gnn_Ws, L3_gnn_bs, L3_gnn_gammas, L3_gnn_betas), axis=-1)
    return x

_drawn_inputs = setup_inputs


def setup_inputs(seed=0):
    import zlib

    import numpy as np

    out = dict(_drawn_inputs(seed))
    spreads = {'L0_gnn_b1': (0.0, 0.1),
     'L0_gnn_b2': (0.0, 0.1),
     'L0_gnn_gamma': (1.0, 0.2),
     'L0_gnn_beta': (0.0, 0.1),
     'L2_gnn_b1': (0.0, 0.1),
     'L2_gnn_b2': (0.0, 0.1),
     'L3_gnn_bs': (0.0, 0.1),
     'L3_gnn_gammas': (1.0, 0.2),
     'L3_gnn_betas': (0.0, 0.1)}
    factors = {}
    for name, (base, spread) in spreads.items():
        noise = np.random.default_rng([zlib.crc32(name.encode()), seed]).standard_normal(out[name].shape)
        drawn = base * np.exp(spread * noise) if base else spread * noise
        out[name] = jnp.asarray(drawn.astype(out[name].dtype))
    for name, factor in factors.items():
        out[name] = (out[name] * factor).astype(out[name].dtype)
    return out
```

```python
from contextlib import ExitStack

import concourse.bass as bass
from concourse import mybir

F32 = mybir.dt.float32
U8 = mybir.dt.uint8
ALU = mybir.AluOpType
ACT = mybir.ActivationFunctionType
AX = mybir.AxisListType

P = 128
EPS = 1e-5
BLOCK_UNITS = 4
COLS = BLOCK_UNITS * P
DUO_UNITS = 2 * BLOCK_UNITS
SLOTS = P // DUO_UNITS
HALF = SLOTS // 2
ROWS = HALF // 2
LAG = 14
LAYERS = 3
WEIGHT_LOADS = 16 * (15 + 4 * LAYERS)
SQ_RING = 4
CB_RING = 4
DVE_UNITS = 3

FINE = 12
TAIL_SLOT = 12
DEV_AT, INV_AT = 4, 6


def unit_of(t, n):
    half, b = t // HALF, 2 * (t % HALF) + n // BLOCK_UNITS
    return 64 * half + 16 * (b % 4) + 4 * (b // 4) + n % BLOCK_UNITS


AT = {}


def place(name, slot, fine):
    AT[name] = slot * FINE + fine


for _name, _slot, _fine in [
    ("adj_turn", 0, 2), ("adj_turned", 0, 8), ("adj_loop", 0, 4), ("adj_keep", 1, 6),
    ("row_sum", 0, 3), ("degree", 0, 5), ("degree_root", 0, 7), ("inv_degree", 0, 10), ("inv_degree2", 1, 0),
    ("has_degree", 1, 2), ("x_bias", 0, 8), ("x_base", 1, 0),
    ("g_keep", 1, 11), ("l0_mm", 2, 1), ("l0_sum", 2, 6), ("ln0", 2, 7),
    ("x1_scaled", 3, 4), ("l1_agg", 3, 6), ("l1_agg_keep", 3, 11), ("l1_mm", 4, 1),
    ("l1_bias", 4, 6), ("l1_relu", 4, 7), ("ln1", 4, 8),
    ("x2_bias", 4, 2), ("x2_base", 5, 6), ("l2_agg", 5, 6), ("l2_agg_keep", 5, 11), ("l2_mm1", 6, 1),
    ("l2_relu", 6, 6), ("l2_mm2", 6, 8), ("l2_sum", 7, 1), ("ln2", 7, 2),
    ("l3_base0", 7, 11), ("l3_agg0", 7, 10), ("l3_agg_keep0", 8, 3), ("l3_mm0", 8, 6),
    ("l3_sum0", 8, 11), ("l3_ln0", 9, 0), ("l3_relu0", 9, 8),
    ("l3_base1", 9, 11), ("l3_agg1", 9, 10), ("l3_agg_keep1", 10, 3), ("l3_mm1", 10, 6),
    ("l3_sum1", 10, 11), ("l3_ln1", 11, 0), ("l3_relu1", 11, 8),
    ("l3_base2", 11, 11), ("l3_agg2", 11, 10), ("l3_agg_keep2", 12, 3), ("l3_mm2", 12, 6),
    ("l3_sum2", 12, 11), ("l3_ln2", 13, 0), ("l3_relu2", 13, 8),
    ("final_sum", 13, 11), ("ln3", 14, 0),
]:
    place(_name, _slot, _fine)


def build(nc, x, adj, nodemask, l0_W1, l0_b1, l0_W2, l0_b2, l0_gamma, l0_beta, l1_W, l1_b,
          l2_W1, l2_b1, l2_W2, l2_b2, l2_eps, l3_Ws, l3_bs, l3_gammas, l3_betas, out):
    G = x.shape[0]
    assert x.shape[1] == x.shape[2] == adj.shape[1] == P

    with ExitStack() as ctx:
        def sb(name, shape, dt=F32):
            return ctx.enter_context(nc.sbuf_tensor(name, shape, dt))

        def ps(name, shape):
            return ctx.enter_context(nc.psum_tensor(name, shape, F32))

        def sem(name):
            return ctx.enter_context(nc.semaphore(name))

        ident = sb("ident", [P, P])
        ident_eps = sb("ident_eps", [P, P])
        sel = sb("sel", [P, 32 + ROWS - 1])
        w1a, w1b = sb("w1a", [P, P]), sb("w1b", [P, P])
        b1_col = sb("b1_col", [P, 1])
        w2 = sb("w2", [P, P])
        w2_mean = sb("w2_mean", [P, 1])
        w2c, w2cg = sb("w2c", [P, P]), sb("w2cg", [P, P])
        b2_row, b2_col = sb("b2_row", [P, P]), sb("b2_col", [P, 1])
        b2_mean = sb("b2_mean", [P, 1])
        b2c_col = sb("b2c_col", [P, 1])
        gamma0, beta0 = sb("gamma0", [P, P]), sb("beta0", [P, P])
        b2cg = sb("b2cg", [P, P])
        l1w, l1wT, l1b = sb("l1w", [P, P]), sb("l1wT", [P, P]), sb("l1b", [P, P])
        l2w1, l2w2 = sb("l2w1", [P, P]), sb("l2w2", [P, P])
        l2b1 = sb("l2b1", [P, 1])
        l2b2 = sb("l2b2", [P, P])
        l2eps = sb("l2eps", [P, 1])
        l3w = sb("l3w", [P, LAYERS, P])
        l3b, l3g, l3beta = sb("l3b", [P, LAYERS, P]), sb("l3g", [P, LAYERS, P]), sb("l3beta", [P, LAYERS, P])
        mask_u8, mask_f = sb("mask_u8", [G, P], U8), sb("mask_f", [G, P])
        mask_all = sb("mask_all", [P, G])

        spare = sb("spare", [P, 1])

        x_in, xT = sb("x_in", [P, P]), sb("xT", [P, P])
        uT, vT = sb("uT", [P, P]), sb("vT", [P, P])
        h = sb("h", [P, SLOTS, DUO_UNITS * P])
        sq = sb("sq", [P, SQ_RING, DUO_UNITS * P])
        dev_rows = sb("dev_rows", [P, 2, COLS])
        dev_nat, inv_nat = sb("dev_nat", [P, P]), sb("inv_nat", [P, P])
        adj_c, c_nat = sb("adj_c", [P, P]), sb("c_nat", [P, P])
        c_line = sb("c_line", [1, 2, HALF * DUO_UNITS * P])
        cb = sb("cb", [P, CB_RING, DUO_UNITS * P])
        gT, gT_keep = sb("gT", [P, P]), sb("gT_keep", [P, P])

        adj_in, x_res = sb("adj_in", [P, P]), sb("x_res", [P, P])
        adjT, adj_self, adj_m = sb("adjT", [P, P]), sb("adj_self", [P, P]), sb("adj_m", [P, P])
        degree, degree_ok, dis = sb("degree", [P, 1]), sb("degree_ok", [P, 1]), sb("dis", [P, 1])
        degree_root = sb("degree_root", [P, 1])
        dis_raw = sb("dis_raw", [P, 1])
        c_sum = sb("c_sum", [P, 1])
        mask_col = sb("mask_col", [P, 1])
        x_bias, x_base = sb("x_bias_t", [P, P]), sb("x_base_t", [P, P])
        x2_bias, x2_base = sb("x2_bias_t", [P, P]), sb("x2_base_t", [P, P])
        z = sb("z", [P, P])
        z_aff = sb("z_aff", [P, P])
        stats, mv, dev, rs = sb("stats", [P, 6]), sb("mv", [P, 2]), sb("dev", [P, 1]), sb("rs", [P, 1])
        x1, x1s, x2, x3 = sb("x1", [P, P]), sb("x1s", [P, P]), sb("x2", [P, P]), sb("x3", [P, P])
        aggT = sb("aggT", [P, P])
        hid2 = sb("hid2", [P, P])
        h3 = sb("h3", [P, P])
        h3_base = sb("h3_base", [P, P])
        x4 = sb("x4", [P, P])

        y_ps = ps("y_ps", [P, 2, DUO_UNITS * P])
        ss_ps = ps("ss_ps", [P, 2, COLS])
        tail_ps = ps("tail_ps", [P, COLS])
        prep_ps = ps("prep_ps", [P, COLS])
        prod = tail_ps[:, 0:P]
        turn_ps, u_ps, v_ps = prep_ps[:, 0:P], prep_ps[:, P:2 * P], prep_ps[:, 2 * P:3 * P]

        weights_in, masks_in = sem("weights_in"), sem("masks_in")
        ones_set, ident_set = sem("ones_set"), sem("ident_set")
        w2_meaned, w2c_set, b2_meaned, b2c_set, affine_set = (
            sem("w2_meaned"), sem("w2c_set"), sem("b2_meaned"), sem("b2c_set"), sem("affine_set"))
        mask_cast, mask_turned, mask_set = sem("mask_cast"), sem("mask_turned"), sem("mask_set")
        wT_turned, wT_set = sem("wT_turned"), sem("wT_set")
        eps_set = sem("eps_set")
        set_up = sem("set_up")
        x_in_in, x_turned, xT_set, uv_made, uv_ready = (
            sem("x_in_in"), sem("x_turned"), sem("xT_set"), sem("uv_made"), sem("uv_ready"))
        h_dve, h_act = sem("h_dve"), sem("h_act")
        y_done, sq_done, ttr_done, bc_done = sem("y_done"), sem("sq_done"), sem("ttr_done"), sem("bc_done")
        var_summed = sem("var_summed")
        adj_c_in = [sem(f"adj_c_in{i}") for i in range(2)]
        dev_nat_in = [sem(f"dev_nat_in{i}") for i in range(2)]
        c_line_in = [sem(f"c_line_in{i}") for i in range(2)]
        dev_done, inv_done, c_done = sem("dev_done"), sem("inv_done"), sem("c_done")
        tail_in, out_stored = sem("tail_in"), sem("out_stored")
        adj_turned, adjT_set, adj_self_set, adj_m_set = (
            sem("adj_turned"), sem("adjT_set"), sem("adj_self_set"), sem("adj_m_set"))
        degree_set, degree_ok_set, degree_root_set, dis_raw_set, dis_set, degree_floor_set = (
            sem("degree_set"), sem("degree_ok_set"), sem("degree_root_set"), sem("dis_raw_set"), sem("dis_set"),
            sem("degree_floor_set"))
        c_sum_set, x_bias_set, x_base_set = sem("c_sum_set"), sem("x_bias_set"), sem("x_base_set")
        mask_col_set, x2_bias_set, x2_base_set = sem("mask_col_set"), sem("x2_bias_set"), sem("x2_base_set")
        g_kept, l0_made = sem("g_kept"), sem("l0_made")
        x1s_set, l1_agged, l1_agg_kept, l1_made, l1_biased = (
            sem("x1s_set"), sem("l1_agged"), sem("l1_agg_kept"), sem("l1_made"), sem("l1_biased"))
        l2_agged, l2_agg_kept, l2_made1, l2_relued, l2_made2 = (
            sem("l2_agged"), sem("l2_agg_kept"), sem("l2_made1"), sem("l2_relued"), sem("l2_made2"))
        l3_based = [sem(f"l3_based{i}") for i in range(LAYERS)]
        l3_agged = [sem(f"l3_agged{i}") for i in range(LAYERS)]
        l3_agg_kept = [sem(f"l3_agg_kept{i}") for i in range(LAYERS)]
        l3_made = [sem(f"l3_made{i}") for i in range(LAYERS)]
        l3_scaled = [sem(f"l3_scaled{i}") for i in range(LAYERS)]
        l3_affined = [sem(f"l3_affined{i}") for i in range(LAYERS)]
        l3_relued = [sem(f"l3_relued{i}") for i in range(LAYERS)]
        NORMS = ["ln0", "ln1", "ln2", "l3_ln0", "l3_ln1", "l3_ln2", "ln3"]
        z_set = {n: sem(f"z_set_{n}") for n in NORMS}
        stats_set = {n: sem(f"stats_set_{n}") for n in NORMS}
        mv_set = {n: sem(f"mv_set_{n}") for n in NORMS}
        dev_set = {n: sem(f"dev_set_{n}") for n in NORMS}
        rs_set = {n: sem(f"rs_set_{n}") for n in NORMS}
        normed = {n: sem(f"normed_{n}") for n in ("ln0", "ln1", "ln2", "ln3")}

        def wait(eng, s, value):
            if isinstance(value, int) and value <= 0:
                return
            eng.wait_ge(s, value)

        def wait_apart(eng, s, value):
            if not isinstance(value, int):
                eng.lower_val(value)
                eng.wait_ge(set_up, 1)
            wait(eng, s, value)

        def program(eng, iteration):
            iteration(new=0, after=1, old=None, older=None)
            iteration(new=1, after=2, old=0, older=None)
            iteration(new=2, after=3, old=1, older=0)
            with eng.Fori(3, G - 1) as g:
                iteration(new=g, after=g + 1, old=g - 1, older=g - 2)
            iteration(new=G - 1, after=None, old=G - 2, older=G - 3)
            iteration(new=None, after=None, old=G - 1, older=G - 2)
            iteration(new=None, after=None, old=None, older=G - 1)

        def tail_graph(s, old, older):
            if s >= TAIL_SLOT:
                return old, (s - TAIL_SLOT) * FINE
            return older, (s + SLOTS - TAIL_SLOT) * FINE

        block = ctx.enter_context(nc.Block())

        @block.sync
        def _(sp):
            def row(v):
                return v.partition_broadcast(P)

            def col(v):
                return v.rearrange("(p o) -> p o", o=1)

            sp.dma_start(x_in[:], x[0]).then_inc(x_in_in, 16)
            WEIGHTS = [
                (w1a[:], l0_W1[0:P, :]), (w1b[:], l0_W1[P:2 * P, :]), (b1_col[:], col(l0_b1)),
                (w2[:], l0_W2), (b2_row[:], row(l0_b2)), (b2_col[:], col(l0_b2)),
                (gamma0[:], row(l0_gamma)), (beta0[:], row(l0_beta)),
                (l1w[:], l1_W), (l1b[:], row(l1_b)),
                (l2w1[:], l2_W1), (l2w2[:], l2_W2), (l2b1[:], col(l2_b1)), (l2b2[:], row(l2_b2)),
                (l2eps[:], row(l2_eps)),
            ]
            for dst, src in WEIGHTS:
                sp.dma_start(dst, src).then_inc(weights_in, 16)
            for i in range(LAYERS):
                sp.dma_start(l3w[:, i, :], l3_Ws[i]).then_inc(weights_in, 16)
                sp.dma_start(l3b[:, i, :], row(l3_bs[i])).then_inc(weights_in, 16)
                sp.dma_start(l3g[:, i, :], row(l3_gammas[i])).then_inc(weights_in, 16)
                sp.dma_start(l3beta[:, i, :], row(l3_betas[i])).then_inc(weights_in, 16)
            sp.dma_start(mask_u8[:], nodemask).then_inc(masks_in, 16)

            def load_adj_c(g, half):
                sp.dma_start(adj_c[64 * half:64 * half + 64, :], adj[g, 64 * half:64 * half + 64, :]
                             ).then_inc(adj_c_in[half], 16)

            def straighten_deviations(g, half):
                wait_apart(sp, dev_done, 2 * g + half + 1)
                wait_apart(sp, inv_done, 2 * (g - 1) + half + 1)
                wait_apart(sp, dev_nat_in[half], 64 * g)
                for q in range(4):
                    i0 = 64 * half + 16 * q
                    sp.dma_start(dev_nat[i0:i0 + 16, :],
                                 dev_rows[32 * q:32 * q + ROWS, half, :].rearrange("p (s j) -> p s j", j=P)
                                 ).then_inc(dev_nat_in[half], 16)

            def line_up_coefficients(g, half):
                wait_apart(sp, c_done, 2 * g + half + 1)
                wait_apart(sp, bc_done, SLOTS * g + HALF * (half - 1))
                wait_apart(sp, c_line_in[half], 16 * g)
                sp.dma_start(c_line[:, half, :].rearrange("o (i j) -> o i j", j=P),
                             c_nat[64 * half:64 * half + 64, :]).then_inc(c_line_in[half], 16)

            load_adj_c(0, 0)
            load_adj_c(0, 1)

            def iteration(new, after, old, older):
                if old is not None:
                    straighten_deviations(old, 1)
                    line_up_coefficients(old, 1)
                    if new is not None:
                        wait_apart(sp, adj_c_in[1], 16 * new)
                        load_adj_c(new, 1)
                    wait_apart(sp, adj_turned, old)
                    wait_apart(sp, adj_self_set, old)
                    wait_apart(sp, adj_m_set, old)
                    wait_apart(sp, degree_set, old)
                    wait_apart(sp, x_base_set, old)
                    wait_apart(sp, tail_in, 32 * old)
                    sp.dma_start(adj_in[:], adj[old]).then_inc(tail_in, 16)
                    sp.dma_start(x_res[:], x[old]).then_inc(tail_in, 16)
                if after is not None:
                    wait_apart(sp, x_turned, new + 1)
                    wait_apart(sp, x_in_in, 16 * (new + 1))
                    sp.dma_start(x_in[:], x[after]).then_inc(x_in_in, 16)
                if new is not None:
                    straighten_deviations(new, 0)
                    line_up_coefficients(new, 0)
                if after is not None:
                    wait_apart(sp, adj_c_in[0], 16 * after)
                    load_adj_c(after, 0)
                if older is not None:
                    wait_apart(sp, normed["ln3"], older + 1)
                    wait_apart(sp, out_stored, 16 * older)
                    sp.dma_start(out[older], x4[:]).then_inc(out_stored, 16)

            program(sp, iteration)
            sp.wait_ge(out_stored, 16 * G)

        @block.tensor
        def _(pe):
            def turn_x(g):
                wait(pe, x_in_in, 16 * (g + 1))
                wait(pe, uv_ready, g)
                wait(pe, adjT_set, g - 2)
                pe.transpose(turn_ps, x_in[:], ident[:]).then_inc(x_turned, 1)

            def make_uv(g):
                wait(pe, xT_set, g + 1)
                pe.matmul(u_ps, w1a[:], xT[:], start=True, stop=True)
                pe.matmul(v_ps, w1b[:], xT[:], start=True, stop=True).then_inc(uv_made, 1)

            def products(g, t, block_of_duo):
                if block_of_duo == 0:
                    wait(pe, h_dve, SLOTS * g + t + 1)
                    wait(pe, h_act, SLOTS * g + t + 1)
                    wait(pe, sq_done, SLOTS * g + t - 1)
                c0 = block_of_duo * COLS
                mm = pe.matmul(y_ps[:, t % 2, c0:c0 + COLS], w2c[:], h[:, t, c0:c0 + COLS], start=True, stop=True)
                if block_of_duo == 1:
                    mm.then_inc(y_done, 1)

            def variances(g, t):
                half, p = t // HALF, (t % HALF) // 2
                wait(pe, sq_done, SLOTS * g + t + 2)
                if p == 0:
                    wait(pe, dev_done, 2 * g + half - 1)
                for q in range(4):
                    c0 = (q % 2) * COLS
                    mm = pe.matmul(ss_ps[32 * q:32 * q + 32, half, :], sel[:, ROWS - 1 - p:ROWS - 1 - p + 32],
                                   sq[:, (t + q // 2) % SQ_RING, c0:c0 + COLS],
                                   start=(p == 0), stop=(p == ROWS - 1))
                mm.then_inc(var_summed, 1)

            def later_layers(g, lo, hi):
                def due(name):
                    return lo <= AT[name] < hi

                if g is None:
                    return
                if due("adj_turn"):
                    wait(pe, tail_in, 32 * (g + 1))
                    pe.transpose(turn_ps, adj_in[:], ident[:]).then_inc(adj_turned, 1)
                if due("l0_mm"):
                    wait(pe, g_kept, g + 1)
                    wait(pe, adjT_set, g + 1)
                    wait(pe, z_set["ln3"], g)
                    pe.matmul(prod, gT_keep[:], w2cg[:], start=True, stop=False)
                    pe.matmul(prod, adjT[:], beta0[:], start=False, stop=True).then_inc(l0_made, 1)
                if due("l1_agg"):
                    wait(pe, x1s_set, g + 1)
                    wait(pe, z_set["ln0"], g + 1)
                    pe.matmul(prod, x1s[:], adjT[:], start=True, stop=True).then_inc(l1_agged, 1)
                if due("l1_mm"):
                    wait(pe, l1_agg_kept, g + 1)
                    pe.matmul(prod, aggT[:], l1wT[:], start=True, stop=True).then_inc(l1_made, 1)
                if due("l2_agg"):
                    wait(pe, normed["ln1"], g + 1)
                    wait(pe, adj_self_set, g + 1)
                    pe.matmul(prod, x2[:], adj_self[:], start=True, stop=True).then_inc(l2_agged, 1)
                if due("l2_mm1"):
                    wait(pe, l2_agg_kept, g + 1)
                    pe.matmul(prod, l2w1[:], aggT[:], start=True, stop=True).then_inc(l2_made1, 1)
                if due("l2_mm2"):
                    wait(pe, l2_relued, g + 1)
                    pe.matmul(prod, hid2[:], l2w2[:], start=True, stop=True).then_inc(l2_made2, 1)
                for i in range(LAYERS):
                    if due(f"l3_agg{i}"):
                        if i == 0:
                            wait(pe, normed["ln2"], g + 1)
                            wait(pe, adj_m_set, g + 1)
                        else:
                            wait(pe, l3_relued[i - 1], g + 1)
                        pe.matmul(prod, (x3 if i == 0 else h3)[:], adj_m[:], start=True, stop=True
                                  ).then_inc(l3_agged[i], 1)
                    if due(f"l3_mm{i}"):
                        wait(pe, l3_agg_kept[i], g + 1)
                        pe.matmul(prod, aggT[:], l3w[:, i, :], start=True, stop=True).then_inc(l3_made[i], 1)

            pe.wait_ge(ident_set, 1)
            pe.wait_ge(weights_in, WEIGHT_LOADS)
            pe.transpose(prod, l1w[:], ident[:]).then_inc(wT_turned, 1)
            pe.wait_ge(mask_cast, 1)
            pe.transpose(turn_ps[:, 0:G], mask_f[:], ident[0:G, 0:G]).then_inc(mask_turned, 1)
            pe.wait_ge(mask_set, 1)
            pe.wait_ge(wT_set, 1)
            turn_x(0)
            make_uv(0)
            pe.wait_ge(w2c_set, 1)
            pe.wait_ge(affine_set, 2)
            pe.wait_ge(ones_set, 3)

            def iteration(new, after, old, older):
                for s in range(SLOTS):
                    g, place0 = tail_graph(s, old, older)
                    yg, t = (new, s - 1) if s >= 1 else (old, SLOTS - 1)
                    if yg is not None:
                        products(yg, t, 0)
                    if s == 9 and after is not None:
                        turn_x(after)
                    later_layers(g, place0, place0 + FINE // 2)
                    if yg is not None:
                        products(yg, t, 1)
                    if s == 10 and after is not None:
                        make_uv(after)
                    later_layers(g, place0 + FINE // 2, place0 + FINE)
                    sg, t = (new, s - 3) if s >= 3 else (old, s + SLOTS - 3)
                    if s % 2 == 1 and sg is not None:
                        variances(sg, t)

            program(pe, iteration)

        @block.scalar
        def _(act):
            def keep_xT(g):
                wait(act, x_turned, g + 1)
                wait(act, uv_made, g)
                act.activation(xT[:], turn_ps, ACT.Copy).then_inc(xT_set, 1)

            def keep_uv(g):
                wait(act, uv_made, g + 1)
                wait(act, h_dve, SLOTS * g)
                wait(act, h_act, SLOTS * g)
                act.activation(uT[:], u_ps, ACT.Identity, bias=b1_col[:])
                act.activation(vT[:], v_ps, ACT.Copy).then_inc(uv_ready, 1)

            def hidden(g, t, n):
                if n == DVE_UNITS:
                    if t == 0:
                        wait(act, uv_ready, g + 1)
                    wait(act, ttr_done, SLOTS * g + t - SLOTS + 1)
                i = unit_of(t, n)
                op = act.activation(h[:, t, n * P:(n + 1) * P], vT[:], ACT.Relu, bias=uT[:, i:i + 1])
                if n == DUO_UNITS - 1:
                    op.then_inc(h_act, 1)

            def squares(g, t):
                wait(act, y_done, SLOTS * g + t + 1)
                wait(act, var_summed, SLOTS // 2 * g + (t - SQ_RING) // 2 + 1)
                act.activation(sq[:, t % SQ_RING, :], y_ps[:, t % 2, :], ACT.Square, bias=b2c_col[:],
                               scale=float(P) ** -0.5).then_inc(sq_done, 1)

            def deviations(g, half):
                wait(act, var_summed, SLOTS // 2 * g + HALF // 2 * (half + 1))
                wait(act, dev_nat_in[half], 64 * g)
                act.activation(dev_rows[:, half, :], ss_ps[:, half, :], ACT.Sqrt, bias=EPS).then_inc(dev_done, 1)

            def later_layers(g, lo, hi):
                def due(name):
                    return lo <= AT[name] < hi

                if g is None:
                    return
                for name in NORMS:
                    if lo <= AT[name] + DEV_AT < hi:
                        wait(act, mv_set[name], g + 1)
                        act.activation(dev[:], mv[:, 1:2], ACT.Sqrt, bias=EPS).then_inc(dev_set[name], 1)
                if due("degree_root"):
                    wait(act, degree_set, g + 1)
                    wait(act, dis_raw_set, g)
                    act.activation(degree_root[:], degree[:], ACT.Sqrt).then_inc(degree_root_set, 1)
                if due("adj_turned"):
                    wait(act, adj_turned, g + 1)
                    wait(act, l1_agged, g)
                    act.activation(adjT[:], turn_ps, ACT.Copy).then_inc(adjT_set, 1)
                if due("l1_agg_keep"):
                    wait(act, l1_agged, g + 1)
                    wait(act, l3_made[LAYERS - 1], g)
                    act.activation(aggT[:], prod, ACT.Copy).then_inc(l1_agg_kept, 1)
                if due("l2_agg_keep"):
                    wait(act, l2_agged, g + 1)
                    act.activation(aggT[:], prod, ACT.Copy).then_inc(l2_agg_kept, 1)
                if due("l2_relu"):
                    wait(act, l2_made1, g + 1)
                    wait(act, l2_made2, g)
                    act.activation(hid2[:], prod, ACT.Relu, bias=l2b1[:]).then_inc(l2_relued, 1)
                for i in range(LAYERS):
                    if due(f"l3_agg_keep{i}"):
                        wait(act, l3_agged[i], g + 1)
                        act.activation(aggT[:], prod, ACT.Copy).then_inc(l3_agg_kept[i], 1)
                    if due(f"l3_relu{i}"):
                        wait(act, l3_affined[i], g + 1)
                        if i == 0:
                            wait(act, z_set["ln3"], g)
                        else:
                            wait(act, l3_based[i], g + 1)
                        act.activation(h3[:], z_aff[:], ACT.Relu).then_inc(l3_relued[i], 1)

            act.wait_ge(weights_in, WEIGHT_LOADS)
            act.wait_ge(wT_turned, 1)
            act.activation(l1wT[:], prod, ACT.Copy).then_inc(wT_set, 1)
            act.wait_ge(mask_turned, 1)
            act.activation(mask_all[:], turn_ps[:, 0:G], ACT.Copy).then_inc(mask_set, 1)
            keep_xT(0)
            keep_uv(0)
            act.wait_ge(b2c_set, 1)

            def iteration(new, after, old, older):
                for s in range(SLOTS):
                    if s == 2 and old is not None:
                        deviations(old, 1)
                    if s == 10 and new is not None:
                        deviations(new, 0)
                    g, place0 = tail_graph(s, old, older)
                    step = FINE // (DUO_UNITS - DVE_UNITS + 1)
                    for k, n in enumerate(range(DVE_UNITS, DUO_UNITS)):
                        if new is not None:
                            hidden(new, s, n)
                        later_layers(g, place0 + k * step, place0 + (k + 1) * step)
                        if k == 1 and s == 10 and after is not None:
                            keep_xT(after)
                    sg, t = (new, s - 1) if s >= 1 else (old, SLOTS - 1)
                    if sg is not None:
                        squares(sg, t)
                    later_layers(g, place0 + (DUO_UNITS - DVE_UNITS) * step, place0 + FINE)
                    if s == SLOTS - 1 and after is not None:
                        keep_uv(after)

            program(act, iteration)

        @block.vector
        def _(dve):
            def hidden(g, t, n):
                if n == 0:
                    if t == 0:
                        wait(dve, uv_ready, g + 1)
                    wait(dve, ttr_done, SLOTS * g + t - SLOTS + 1)
                i = unit_of(t, n)
                op = dve.tensor_scalar(h[:, t, n * P:(n + 1) * P], vT[:], uT[:, i:i + 1], 0.0, ALU.add, ALU.max)
                if n == DVE_UNITS - 1:
                    op.then_inc(h_dve, 1)

            def weighted_sum(g, t, n):
                if n == 0:
                    wait(dve, bc_done, SLOTS * g + t + 1)
                    if t == 0:
                        wait(dve, g_kept, g)
                i = unit_of(t, n)
                cols = slice(n * P, (n + 1) * P)
                op = dve.tensor_tensor_reduce(h[:, t, cols], h[:, t, cols], cb[:, t % CB_RING, cols], 1.0, 0.0,
                                              ALU.mult, ALU.add, gT[:, i:i + 1])
                if n == DUO_UNITS - 1:
                    op.then_inc(ttr_done, 1)

            def invert(g, half):
                rows = slice(64 * half, 64 * half + 64)
                wait(dve, dev_nat_in[half], 64 * (g + 1))
                wait(dve, c_done, 2 * (g - 1) + half + 1)
                dve.reciprocal(inv_nat[rows, :], dev_nat[rows, :]).then_inc(inv_done, 1)

            def sum_coefficients(g):
                wait(dve, c_done, 2 * (g + 1))
                wait(dve, x_bias_set, g)
                dve.tensor_reduce(c_sum[:], c_nat[:], AX.X, ALU.add).then_inc(c_sum_set, 1)

            def norm_steps(g, name, lo, hi):
                at = AT[name]
                if lo <= at < hi:
                    wait(dve, z_set[name], g + 1)
                    dve.bn_stats(stats[:], z[:]).then_inc(stats_set[name], 1)
                if lo <= at + 1 < hi:
                    wait_apart(dve, stats_set[name], g + 1)
                    dve.bn_aggr(mv[:], stats[:]).then_inc(mv_set[name], 1)
                if lo <= at + INV_AT < hi:
                    wait(dve, dev_set[name], g + 1)
                    dve.reciprocal(rs[:], dev[:]).then_inc(rs_set[name], 1)

            def norm(g, name, dst, lo, hi):
                norm_steps(g, name, lo, hi)
                if lo <= AT[name] + INV_AT + 1 < hi:
                    wait(dve, rs_set[name], g + 1)
                    dve.tensor_scalar(dst[:], z[:], mv[:, 0:1], rs[:], ALU.subtract, ALU.mult
                                      ).then_inc(normed[name], 1)

            def later_layers(g, lo, hi):
                def due(name):
                    return lo <= AT[name] < hi

                if g is None:
                    return
                if due("row_sum"):
                    wait(dve, tail_in, 32 * (g + 1))
                    dve.tensor_reduce(degree[:], adj_in[:], AX.X, ALU.add).then_inc(degree_set, 1)
                if due("degree"):
                    wait(dve, degree_set, g + 1)
                    dve.tensor_scalar(degree_ok[:], degree[:], 0.0, None, ALU.is_gt).then_inc(degree_ok_set, 1)
                if due("inv_degree"):
                    wait(dve, degree_root_set, g + 1)
                    dve.tensor_scalar(degree_root[:], degree_root[:], 1e-38, None, ALU.max).then_inc(degree_floor_set, 1)
                if due("inv_degree2"):
                    wait(dve, degree_floor_set, g + 1)
                    dve.reciprocal(dis_raw[:], degree_root[:]).then_inc(dis_raw_set, 1)
                if due("has_degree"):
                    wait(dve, degree_ok_set, g + 1)
                    wait(dve, dis_raw_set, g + 1)
                    wait(dve, x1s_set, g)
                    dve.tensor_tensor(dis[:], dis_raw[:], degree_ok[:], ALU.mult).then_inc(dis_set, 1)
                if due("g_keep"):
                    wait(dve, ttr_done, SLOTS * (g + 1))
                    wait(dve, l0_made, g)
                    dve.tensor_copy(gT_keep[:], gT[:]).then_inc(g_kept, 1)
                if due("l0_sum"):
                    wait(dve, l0_made, g + 1)
                    wait(dve, x_base_set, g + 1)
                    dve.tensor_tensor(z[:], prod, x_base[:], ALU.add).then_inc(z_set["ln0"], 1)
                norm(g, "ln0", x1, lo, hi)
                if due("l1_bias"):
                    wait(dve, l1_made, g + 1)
                    dve.scalar_tensor_tensor(out=z_aff[:], in0=prod, scalar=dis[:], in1=l1b[:],
                                             op0=ALU.mult, op1=ALU.add).then_inc(l1_biased, 1)
                if due("l1_relu"):
                    wait(dve, l1_biased, g + 1)
                    dve.scalar_tensor_tensor(out=z[:], in0=z_aff[:], scalar=0.0, in1=x1[:],
                                             op0=ALU.max, op1=ALU.add).then_inc(z_set["ln1"], 1)
                norm(g, "ln1", x2, lo, hi)
                if due("l2_sum"):
                    wait(dve, l2_made2, g + 1)
                    wait(dve, x2_base_set, g + 1)
                    dve.scalar_tensor_tensor(out=z[:], in0=prod, scalar=mask_col[:], in1=x2_base[:],
                                             op0=ALU.mult, op1=ALU.add).then_inc(z_set["ln2"], 1)
                norm(g, "ln2", x3, lo, hi)
                for i in range(LAYERS):
                    name = f"l3_ln{i}"
                    if due(f"l3_sum{i}"):
                        wait(dve, l3_made[i], g + 1)
                        wait(dve, l3_based[i], g + 1)
                        dve.tensor_tensor(z[:], prod, h3_base[:], ALU.add).then_inc(z_set[name], 1)
                    norm_steps(g, name, lo, hi)
                    if lo <= AT[name] + 2 < hi:
                        wait(dve, mv_set[name], g + 1)
                        if i > 0:
                            wait(dve, l3_relued[i - 1], g + 1)
                        else:
                            wait(dve, z_set["ln1"], g + 1)
                        dve.scalar_tensor_tensor(out=z_aff[:], in0=z[:], scalar=mv[:, 0:1], in1=l3g[:, i, :],
                                                 op0=ALU.subtract, op1=ALU.mult).then_inc(l3_scaled[i], 1)
                    if lo <= AT[name] + INV_AT + 1 < hi:
                        wait(dve, l3_scaled[i], g + 1)
                        wait(dve, rs_set[name], g + 1)
                        dve.scalar_tensor_tensor(out=z_aff[:], in0=z_aff[:], scalar=rs[:], in1=l3beta[:, i, :],
                                                 op0=ALU.mult, op1=ALU.add).then_inc(l3_affined[i], 1)
                if due("final_sum"):
                    wait(dve, l3_relued[LAYERS - 1], g + 1)
                    dve.tensor_tensor(z[:], h3[:], x3[:], ALU.add).then_inc(z_set["ln3"], 1)
                if lo <= AT["ln3"] + INV_AT + 1 < hi:
                    wait(dve, out_stored, 16 * g)
                norm(g, "ln3", x4, lo, hi)

            dve.wait_ge(weights_in, WEIGHT_LOADS)
            dve.tensor_reduce(w2_mean[:], w2[:], AX.X, ALU.add).then_inc(w2_meaned, 1)
            dve.tensor_reduce(b2_mean[:], b2_row[:], AX.X, ALU.add).then_inc(b2_meaned, 1)
            dve.wait_ge(w2_meaned, 1)
            dve.tensor_scalar(w2_mean[:], w2_mean[:], 1.0 / P, None, ALU.mult).then_inc(w2_meaned, 1)
            dve.wait_ge(b2_meaned, 1)
            dve.tensor_scalar(b2_mean[:], b2_mean[:], 1.0 / P, None, ALU.mult).then_inc(b2_meaned, 1)
            dve.wait_ge(w2_meaned, 2)
            dve.tensor_scalar(w2c[:], w2[:], w2_mean[:], None, ALU.subtract).then_inc(w2c_set, 1)
            dve.wait_ge(b2_meaned, 2)
            dve.tensor_scalar(b2c_col[:], b2_col[:], b2_mean[:], float(P) ** -0.5, ALU.subtract, ALU.mult
                              ).then_inc(b2c_set, 1)
            dve.wait_ge(w2c_set, 1)
            dve.tensor_tensor(w2cg[:], w2c[:], gamma0[:], ALU.mult).then_inc(affine_set, 1)
            dve.scalar_tensor_tensor(out=b2cg[:], in0=b2_row[:], scalar=b2_mean[:], in1=gamma0[:],
                                     op0=ALU.subtract, op1=ALU.mult).then_inc(affine_set, 1)
            dve.wait_ge(masks_in, 16)
            dve.tensor_copy(mask_f[:], mask_u8[:]).then_inc(mask_cast, 1)
            dve.tensor_scalar(l2eps[:], l2eps[:], 1.0, None, ALU.add).then_inc(eps_set, 1)
            dve.wait_ge(eps_set, 1)
            dve.wait_ge(ident_set, 1)
            dve.tensor_scalar(ident_eps[:], ident[:], l2eps[:], None, ALU.mult).then_inc(eps_set, 1)

            def iteration(new, after, old, older):
                for s in range(SLOTS):
                    g, place0 = tail_graph(s, old, older)
                    wg, t = (new, s - LAG) if s >= LAG else (old, s + SLOTS - LAG)
                    for k in range(DVE_UNITS + DUO_UNITS):
                        if k < DVE_UNITS and new is not None:
                            hidden(new, s, k)
                        if k >= DVE_UNITS and wg is not None:
                            weighted_sum(wg, t, k - DVE_UNITS)
                        last = k == DVE_UNITS + DUO_UNITS - 1
                        later_layers(g, place0 + k, place0 + (FINE if last else k + 1))
                    if s == 3 and old is not None:
                        invert(old, 1)
                    if s == 6 and old is not None:
                        sum_coefficients(old)
                    if s == 11 and new is not None:
                        invert(new, 0)

            program(dve, iteration)

        @block.gpsimd
        def _(pool):
            def coefficients(g, half):
                rows = slice(64 * half, 64 * half + 64)
                if half == 1:
                    wait_apart(pool, bc_done, SLOTS * (g + 1) + 4 - LAG + 2)
                wait(pool, inv_done, 2 * g + half + 1)
                wait(pool, adj_c_in[half], 16 * (g + 1))
                wait(pool, c_line_in[half], 16 * g)
                wait(pool, c_sum_set, g)
                pool.tensor_tensor(c_nat[rows, :], adj_c[rows, :], inv_nat[rows, :], ALU.mult).then_inc(c_done, 1)
                if half == 1:
                    wait_apart(pool, c_done, 2 * (g + 1))

            def broadcast(g, t):
                half = t // HALF
                if t % HALF == 0:
                    wait_apart(pool, c_line_in[half], 16 * (g + 1))
                wait_apart(pool, ttr_done, SLOTS * g + t + 1 - CB_RING)
                p, q = (t % HALF) // 2, 2 * (t % 2)
                blocks = c_line[:, half, :].rearrange("o (q p n) -> o q p n", q=4, p=ROWS)[:, q:q + 2, p, :]
                pool.partition_broadcast(cb[:, t % CB_RING, :].rearrange("c (q n) -> c q n", q=2), blocks,
                                         channels=P).then_inc(bc_done, 1)

            def later_layers(g, lo, hi):
                def due(name):
                    return lo <= AT[name] < hi

                if g is None:
                    return
                if due("adj_loop"):
                    wait(pool, tail_in, 32 * (g + 1))
                    wait(pool, l2_agged, g)
                    pool.tensor_tensor(adj_self[:], adj_in[:], ident_eps[:], ALU.add).then_inc(adj_self_set, 1)
                if due("adj_keep"):
                    wait_apart(pool, l3_agged[LAYERS - 1], g)
                    pool.tensor_copy(adj_m[:], adj_in[:]).then_inc(adj_m_set, 1)
                    wait_apart(pool, x2_bias_set, g)
                    wait_apart(pool, z_set["ln2"], g)
                    pool.tensor_copy(mask_col[:], mask_all[:, g:g + 1] if isinstance(g, int)
                                     else mask_all[:, bass.ds(g, 1)]).then_inc(mask_col_set, 1)
                if due("x_bias"):
                    wait(pool, c_sum_set, g + 1)
                    pool.tensor_tensor(x_bias[:], b2cg[:], c_sum[:].to_broadcast([P, P]), ALU.mult
                                       ).then_inc(x_bias_set, 1)
                if due("x_base"):
                    wait(pool, x_bias_set, g + 1)
                    wait(pool, z_set["ln0"], g)
                    pool.tensor_tensor(x_base[:], x_bias[:], x_res[:], ALU.add).then_inc(x_base_set, 1)
                if due("x1_scaled"):
                    wait(pool, normed["ln0"], g + 1)
                    wait(pool, dis_set, g + 1)
                    pool.tensor_tensor(x1s[:], x1[:], dis[:].to_broadcast([P, P]), ALU.mult).then_inc(x1s_set, 1)
                if due("x2_bias"):
                    wait(pool, mask_col_set, g + 1)
                    pool.tensor_tensor(x2_bias[:], l2b2[:], mask_col[:].to_broadcast([P, P]), ALU.mult
                                       ).then_inc(x2_bias_set, 1)
                if due("x2_base"):
                    wait(pool, x2_bias_set, g + 1)
                    wait(pool, normed["ln1"], g + 1)
                    pool.tensor_tensor(x2_base[:], x2_bias[:], x2[:], ALU.add).then_inc(x2_base_set, 1)
                for i in range(LAYERS):
                    if due(f"l3_base{i}"):
                        wait(pool, normed["ln2"] if i == 0 else l3_relued[i - 1], g + 1)
                        if i > 0:
                            wait(pool, z_set[f"l3_ln{i - 1}"], g + 1)
                        pool.tensor_tensor(h3_base[:], (x3 if i == 0 else h3)[:], l3b[:, i, :], ALU.add
                                           ).then_inc(l3_based[i], 1)

            pool.memset(ident[:], 0.0).then_inc(ones_set, 1)
            pool.memset(sel[:], 0.0).then_inc(ones_set, 1)
            pool.wait_ge(ones_set, 2)
            pool.affine_select(out=ident[:], in_=ident[:], compare_op=ALU.not_equal, fill=1.0, base=0,
                               pattern=[[-1, P]], channel_multiplier=1).then_inc(ident_set, 1)
            pool.memset(sel[:, ROWS - 1:ROWS], 1.0).then_inc(ones_set, 1)
            pool.wait_ge(affine_set, 2)
            pool.wait_ge(eps_set, 2)
            pool.wait_ge(mask_set, 1)
            pool.memset(spare[:], 0.0).then_inc(set_up, 1)

            def iteration(new, after, old, older):
                for s in range(SLOTS):
                    g, place0 = tail_graph(s, old, older)
                    later_layers(g, place0, place0 + FINE // 2)
                    bg, t = (new, s - LAG + 1) if s >= LAG - 1 else (old, s + SLOTS - LAG + 1)
                    if s == 12 and new is not None:
                        coefficients(new, 0)
                    if bg is not None:
                        broadcast(bg, t)
                    if s == 4 and old is not None:
                        coefficients(old, 1)
                    later_layers(g, place0 + FINE // 2, place0 + FINE)

            program(pool, iteration)


_INS = ['x', 'adj', 'nodemask', 'L0_gnn_W1', 'L0_gnn_b1', 'L0_gnn_W2', 'L0_gnn_b2', 'L0_gnn_gamma', 'L0_gnn_beta',
        'L1_gnn_W', 'L1_gnn_b', 'L2_gnn_W1', 'L2_gnn_b1', 'L2_gnn_W2', 'L2_gnn_b2', 'L2_gnn_eps',
        'L3_gnn_Ws', 'L3_gnn_bs', 'L3_gnn_gammas', 'L3_gnn_betas']


def kernel(**inputs):
    import numpy as np
    import concourse.bacc as bacc
    from concourse.bass_utils import run_bass_kernel_spmd

    nc = bacc.Bacc("TRN2", target_bir_lowering=False, num_devices=1)
    arrays, args = {}, []
    for name in _INS:
        a = np.ascontiguousarray(inputs[name])
        arrays[f"in_{name}_dram"] = a
        args.append(nc.dram_tensor(f"in_{name}_dram", a.shape, mybir.dt.from_np(a.dtype), kind="ExternalInput").ap())
    shape = tuple(inputs["x"].shape)
    args.append(nc.dram_tensor("out_dram", shape, F32, kind="ExternalOutput").ap())
    build(nc, *args)
    r = run_bass_kernel_spmd(nc, [arrays], core_ids=[0])
    return r.results[0]["out_dram"]
```

```python
from contextlib import ExitStack

import concourse.bass as bass
from concourse import mybir

F32 = mybir.dt.float32
BF16 = mybir.dt.bfloat16
U8 = mybir.dt.uint8
ALU = mybir.AluOpType
ACT = mybir.ActivationFunctionType
AX = mybir.AxisListType

P = 128
EPS = 1e-5
BLOCK_UNITS = 4
COLS = BLOCK_UNITS * P
DUO_UNITS = 2 * BLOCK_UNITS
SLOTS = P // DUO_UNITS
HALF = SLOTS // 2
ROWS = HALF // 2
LAG = 14
LAYERS = 3
WEIGHT_LOADS = 16 * (15 + 4 * LAYERS)
SQ_RING = 4
PARTS = 3
HALF_BLOCKS = 2 * HALF
DVE_UNITS = 2
POOL_UNITS = DUO_UNITS - DVE_UNITS
PRE_RING = 4

FINE = 12
TAIL_SLOT = 12
DEV_AT, INV_AT = 4, 6
INVERT_STEP = 6


def unit_of(t, n):
    half, b = t // HALF, 2 * (t % HALF) + n // BLOCK_UNITS
    return 64 * half + 16 * (b % 4) + 4 * (b // 4) + n % BLOCK_UNITS


AT = {}


def place(name, slot, fine):
    AT[name] = slot * FINE + fine


for _name, _slot, _fine in [
    ("adj_turn", 0, 2), ("adj_turned", 0, 8), ("adj_loop", 0, 4), ("adj_keep", 1, 6),
    ("row_sum", 0, 3), ("degree", 0, 5), ("degree_root", 0, 7), ("inv_degree", 0, 10), ("inv_degree2", 1, 0),
    ("has_degree", 1, 2), ("x_bias", 0, 8), ("x_base", 1, 0),
    ("g_keep", 1, 11), ("l0_mm", 2, 1), ("l0_sum", 2, 6), ("ln0", 2, 7),
    ("x1_scaled", 3, 4), ("l1_agg", 4, 0), ("l1_agg_keep", 4, 5), ("l1_mm", 4, 6),
    ("l1_bias", 5, 0), ("l1_relu", 5, 1), ("ln1", 5, 2),
    ("x2_bias", 4, 2), ("x2_base", 6, 0), ("l2_agg", 6, 0), ("l2_agg_keep", 6, 5), ("l2_mm1", 6, 7),
    ("l2_relu", 7, 0), ("l2_mm2", 7, 2), ("l2_sum", 7, 7), ("ln2", 7, 8),
    ("l3_base0", 8, 5), ("l3_agg0", 8, 4), ("l3_agg_keep0", 8, 9), ("l3_mm0", 9, 0),
    ("l3_sum0", 9, 5), ("l3_ln0", 9, 6), ("l3_relu0", 10, 2),
    ("l3_base1", 10, 5), ("l3_agg1", 10, 4), ("l3_agg_keep1", 10, 9), ("l3_mm1", 11, 0),
    ("l3_sum1", 11, 5), ("l3_ln1", 11, 6), ("l3_relu1", 12, 2),
    ("l3_base2", 12, 5), ("l3_agg2", 12, 4), ("l3_agg_keep2", 12, 9), ("l3_mm2", 12, 10),
    ("l3_sum2", 13, 3), ("l3_ln2", 13, 4), ("l3_relu2", 14, 0),
    ("final_sum", 14, 3), ("ln3", 14, 4),
]:
    place(_name, _slot, _fine)


def build(nc, x, adj, nodemask, l0_W1, l0_b1, l0_W2, l0_b2, l0_gamma, l0_beta, l1_W, l1_b,
          l2_W1, l2_b1, l2_W2, l2_b2, l2_eps, l3_Ws, l3_bs, l3_gammas, l3_betas, out):
    G = x.shape[0]
    assert x.shape[1] == x.shape[2] == adj.shape[1] == P

    with ExitStack() as ctx:
        def sb(name, shape, dt=F32):
            return ctx.enter_context(nc.sbuf_tensor(name, shape, dt))

        def ps(name, shape):
            return ctx.enter_context(nc.psum_tensor(name, shape, F32))

        def sem(name):
            return ctx.enter_context(nc.semaphore(name))

        ident = sb("ident", [P, P])
        ident_eps = sb("ident_eps", [P, P])
        sel = sb("sel", [P, 32 + ROWS - 1])
        w1a, w1b = sb("w1a", [P, P]), sb("w1b", [P, P])
        b1_col = sb("b1_col", [P, 1])
        w2 = sb("w2", [P, P])
        w2_mean = sb("w2_mean", [P, 1])
        w2c, w2cg = sb("w2c", [P, P]), sb("w2cg", [P, P])
        b2_row, b2_col = sb("b2_row", [P, P]), sb("b2_col", [P, 1])
        b2_mean = sb("b2_mean", [P, 1])
        b2c_col = sb("b2c_col", [P, 1])
        gamma0, beta0 = sb("gamma0", [P, P]), sb("beta0", [P, P])
        b2cg = sb("b2cg", [P, P])
        l1w, l1wT, l1b = sb("l1w", [P, P]), sb("l1wT", [P, P]), sb("l1b", [P, P])
        l2w1, l2w2 = sb("l2w1", [P, P]), sb("l2w2", [P, P])
        l2b1 = sb("l2b1", [P, 1])
        l2b2 = sb("l2b2", [P, P])
        l2eps = sb("l2eps", [P, 1])
        l3w = sb("l3w", [P, LAYERS, P])
        l3b, l3g, l3beta = sb("l3b", [P, LAYERS, P]), sb("l3g", [P, LAYERS, P]), sb("l3beta", [P, LAYERS, P])
        mask_u8, mask_f = sb("mask_u8", [G, P], U8), sb("mask_f", [G, P])
        mask_all = sb("mask_all", [P, G])

        x_in, xT = sb("x_in", [P, P]), sb("xT", [P, P])
        uT, vT = sb("uT", [P, P]), sb("vT", [P, P])
        h = sb("h", [P, SLOTS, DUO_UNITS * P])
        pre = sb("pre", [P, PRE_RING, POOL_UNITS * P])
        sq = sb("sq", [P, SQ_RING, DUO_UNITS * P])
        dev_rows = sb("dev_rows", [P, 2, COLS])
        dev_nat, inv_nat = sb("dev_nat", [P, P]), sb("inv_nat", [P, P])
        adj_c, c_nat = sb("adj_c", [P, P]), sb("c_nat", [P, P])
        c_rest = sb("c_rest", [P, P])
        c_part = [sb(f"c_part{k}", [P, P], BF16) for k in range(PARTS)]
        c_rows = sb("c_rows", [32 * PARTS, 2, COLS], BF16)
        pick = sb("pick", [32 * PARTS, HALF_BLOCKS, P], BF16)
        gT, gT_keep = sb("gT", [P, P]), sb("gT_keep", [P, P])

        adj_in, x_res = sb("adj_in", [P, P]), sb("x_res", [P, P])
        adjT, adj_self, adj_m = sb("adjT", [P, P]), sb("adj_self", [P, P]), sb("adj_m", [P, P])
        degree, degree_ok, dis = sb("degree", [P, 1]), sb("degree_ok", [P, 1]), sb("dis", [P, 1])
        degree_root = sb("degree_root", [P, 1])
        dis_raw = sb("dis_raw", [P, 1])
        c_sum = sb("c_sum", [P, 1])
        mask_col = sb("mask_col", [P, 1])
        x_bias, x_base = sb("x_bias_t", [P, P]), sb("x_base_t", [P, P])
        x2_bias, x2_base = sb("x2_bias_t", [P, P]), sb("x2_base_t", [P, P])
        z = sb("z", [P, P])
        z_aff = sb("z_aff", [P, P])
        stats, mv, dev, rs = sb("stats", [P, 6]), sb("mv", [P, 2]), sb("dev", [P, 1]), sb("rs", [P, 1])
        x1, x1s, x2, x3 = sb("x1", [P, P]), sb("x1s", [P, P]), sb("x2", [P, P]), sb("x3", [P, P])
        aggT = sb("aggT", [P, P])
        hid2 = sb("hid2", [P, P])
        h3 = sb("h3", [P, P])
        h3_base = sb("h3_base", [P, P])
        x4 = sb("x4", [P, P])

        y_ps = ps("y_ps", [P, 2, DUO_UNITS * P])
        ss_ps = ps("ss_ps", [P, COLS])
        cb_ps = ps("cb_ps", [P, 2, COLS])
        small_ps = ps("small_ps", [P, 4, P])
        prod, turn_ps, u_ps, v_ps = (small_ps[:, i, :] for i in range(4))

        weights_in, masks_in = sem("weights_in"), sem("masks_in")
        ones_set, ident_set = sem("ones_set"), sem("ident_set")
        w2_meaned, w2c_set, b2_meaned, b2c_set, affine_set = (
            sem("w2_meaned"), sem("w2c_set"), sem("b2_meaned"), sem("b2c_set"), sem("affine_set"))
        mask_cast, mask_turned, mask_set = sem("mask_cast"), sem("mask_turned"), sem("mask_set")
        wT_turned, wT_set = sem("wT_turned"), sem("wT_set")
        eps_set = sem("eps_set")
        set_up, pick_set = sem("set_up"), sem("pick_set")
        x_in_in, x_turned, xT_set, uv_made, uv_ready = (
            sem("x_in_in"), sem("x_turned"), sem("xT_set"), sem("uv_made"), sem("uv_ready"))
        pre_made, h_dve, h_act = sem("pre_made"), sem("h_dve"), sem("h_act")
        y_done, sq_done = sem("y_done"), sem("sq_done")
        bc_done, ttr_done = sem("bc_done"), sem("ttr_done")
        var_summed = sem("var_summed")
        adj_c_in = sem("adj_c_in")
        dev_nat_in = [sem(f"dev_nat_in{i}") for i in range(2)]
        c_rows_in = [sem(f"c_rows_in{i}") for i in range(2)]
        dev_done, inv_done, c_made = sem("dev_done"), sem("inv_done"), sem("c_made")
        part_done = [sem(f"part_done{k}") for k in range(PARTS)]
        rest_done = sem("rest_done")
        tail_in, out_stored = sem("tail_in"), sem("out_stored")
        adj_turned, adjT_set, adj_self_set, adj_m_set = (
            sem("adj_turned"), sem("adjT_set"), sem("adj_self_set"), sem("adj_m_set"))
        degree_set, degree_ok_set, degree_root_set, dis_raw_set, dis_set, degree_floor_set = (
            sem("degree_set"), sem("degree_ok_set"), sem("degree_root_set"), sem("dis_raw_set"), sem("dis_set"),
            sem("degree_floor_set"))
        c_sum_set, x_bias_set, x_base_set = sem("c_sum_set"), sem("x_bias_set"), sem("x_base_set")
        mask_col_set, x2_bias_set, x2_base_set = sem("mask_col_set"), sem("x2_bias_set"), sem("x2_base_set")
        g_kept, l0_made = sem("g_kept"), sem("l0_made")
        x1s_set, l1_agged, l1_agg_kept, l1_made, l1_biased = (
            sem("x1s_set"), sem("l1_agged"), sem("l1_agg_kept"), sem("l1_made"), sem("l1_biased"))
        l2_agged, l2_agg_kept, l2_made1, l2_relued, l2_made2 = (
            sem("l2_agged"), sem("l2_agg_kept"), sem("l2_made1"), sem("l2_relued"), sem("l2_made2"))
        l3_based = [sem(f"l3_based{i}") for i in range(LAYERS)]
        l3_agged = [sem(f"l3_agged{i}") for i in range(LAYERS)]
        l3_agg_kept = [sem(f"l3_agg_kept{i}") for i in range(LAYERS)]
        l3_made = [sem(f"l3_made{i}") for i in range(LAYERS)]
        l3_scaled = [sem(f"l3_scaled{i}") for i in range(LAYERS)]
        l3_affined = [sem(f"l3_affined{i}") for i in range(LAYERS)]
        l3_relued = [sem(f"l3_relued{i}") for i in range(LAYERS)]
        NORMS = ["ln0", "ln1", "ln2", "l3_ln0", "l3_ln1", "l3_ln2", "ln3"]
        z_set = {n: sem(f"z_set_{n}") for n in NORMS}
        stats_set = {n: sem(f"stats_set_{n}") for n in NORMS}
        mv_set = {n: sem(f"mv_set_{n}") for n in NORMS}
        dev_set = {n: sem(f"dev_set_{n}") for n in NORMS}
        rs_set = {n: sem(f"rs_set_{n}") for n in NORMS}
        normed = {n: sem(f"normed_{n}") for n in ("ln0", "ln1", "ln2", "ln3")}

        def wait(eng, s, value):
            if isinstance(value, int) and value <= 0:
                return
            eng.wait_ge(s, value)

        def wait_apart(eng, s, value):
            if not isinstance(value, int):
                eng.lower_val(value)
                eng.wait_ge(set_up, 1)
            wait(eng, s, value)

        def program(eng, iteration):
            iteration(new=0, after=1, old=None, older=None)
            iteration(new=1, after=2, old=0, older=None)
            iteration(new=2, after=3, old=1, older=0)
            with eng.Fori(3, G - 1) as g:
                iteration(new=g, after=g + 1, old=g - 1, older=g - 2)
            iteration(new=G - 1, after=None, old=G - 2, older=G - 3)
            iteration(new=None, after=None, old=G - 1, older=G - 2)
            iteration(new=None, after=None, old=None, older=G - 1)

        def tail_graph(s, old, older):
            if s >= TAIL_SLOT:
                return old, (s - TAIL_SLOT) * FINE
            return older, (s + SLOTS - TAIL_SLOT) * FINE

        block = ctx.enter_context(nc.Block())

        @block.sync
        def _(sp):
            def row(v):
                return v.partition_broadcast(P)

            def col(v):
                return v.rearrange("(p o) -> p o", o=1)

            sp.dma_start(x_in[:], x[0]).then_inc(x_in_in, 16)
            WEIGHTS = [
                (w1a[:], l0_W1[0:P, :]), (w1b[:], l0_W1[P:2 * P, :]), (b1_col[:], col(l0_b1)),
                (w2[:], l0_W2), (b2_row[:], row(l0_b2)), (b2_col[:], col(l0_b2)),
                (gamma0[:], row(l0_gamma)), (beta0[:], row(l0_beta)),
                (l1w[:], l1_W), (l1b[:], row(l1_b)),
                (l2w1[:], l2_W1), (l2w2[:], l2_W2), (l2b1[:], col(l2_b1)), (l2b2[:], row(l2_b2)),
                (l2eps[:], row(l2_eps)),
            ]
            for dst, src in WEIGHTS:
                sp.dma_start(dst, src).then_inc(weights_in, 16)
            for i in range(LAYERS):
                sp.dma_start(l3w[:, i, :], l3_Ws[i]).then_inc(weights_in, 16)
                sp.dma_start(l3b[:, i, :], row(l3_bs[i])).then_inc(weights_in, 16)
                sp.dma_start(l3g[:, i, :], row(l3_gammas[i])).then_inc(weights_in, 16)
                sp.dma_start(l3beta[:, i, :], row(l3_betas[i])).then_inc(weights_in, 16)
            sp.dma_start(mask_u8[:], nodemask).then_inc(masks_in, 16)

            def load_adj_c(g):
                wait_apart(sp, adj_c_in, 16 * g)
                sp.dma_start(adj_c[:], adj[g]).then_inc(adj_c_in, 16)

            def straighten_deviations(g, half):
                wait_apart(sp, dev_done, 2 * g + half + 1)
                wait_apart(sp, inv_done, 2 * (g - 1) + half + 1)
                wait_apart(sp, dev_nat_in[half], 64 * g)
                for q in range(4):
                    i0 = 64 * half + 16 * q
                    sp.dma_start(dev_nat[i0:i0 + 16, :],
                                 dev_rows[32 * q:32 * q + ROWS, half, :].rearrange("p (s j) -> p s j", j=P)
                                 ).then_inc(dev_nat_in[half], 16)

            def line_up_coefficients(g, half):
                wait_apart(sp, bc_done, 2 * (SLOTS * g + HALF * (half - 1)))
                wait_apart(sp, c_rows_in[half], 48 * g)
                for k in range(PARTS):
                    wait_apart(sp, part_done[k], 2 * g + half + 1)
                    sp.dma_start(c_rows[32 * k:32 * k + HALF_BLOCKS, half, :].rearrange("b (s j) -> b s j", j=P),
                                 c_part[k][64 * half:64 * half + 64, :]).then_inc(c_rows_in[half], 16)

            sp.wait_ge(set_up, 1)
            load_adj_c(0)

            def iteration(new, after, old, older):
                if old is not None:
                    straighten_deviations(old, 1)
                    line_up_coefficients(old, 1)
                    if new is not None:
                        wait_apart(sp, part_done[0], 2 * (old + 1))
                        load_adj_c(new)
                    wait_apart(sp, adj_turned, old)
                    wait_apart(sp, adj_self_set, old)
                    wait_apart(sp, adj_m_set, old)
                    wait_apart(sp, degree_set, old)
                    wait_apart(sp, x_base_set, old)
                    wait_apart(sp, tail_in, 32 * old)
                    sp.dma_start(adj_in[:], adj[old]).then_inc(tail_in, 16)
                    sp.dma_start(x_res[:], x[old]).then_inc(tail_in, 16)
                if after is not None:
                    wait_apart(sp, x_turned, new + 1)
                    wait_apart(sp, x_in_in, 16 * (new + 1))
                    sp.dma_start(x_in[:], x[after]).then_inc(x_in_in, 16)
                if new is not None:
                    straighten_deviations(new, 0)
                    line_up_coefficients(new, 0)
                if older is not None:
                    wait_apart(sp, normed["ln3"], older + 1)
                    wait_apart(sp, out_stored, 16 * older)
                    sp.dma_start(out[older], x4[:]).then_inc(out_stored, 16)

            program(sp, iteration)
            sp.wait_ge(out_stored, 16 * G)

        @block.tensor
        def _(pe):
            def turn_x(g):
                wait(pe, x_in_in, 16 * (g + 1))
                wait(pe, uv_ready, g)
                wait(pe, z_set["l3_ln2"], g - 2)
                pe.transpose(turn_ps, x_in[:], ident[:]).then_inc(x_turned, 1)

            def make_uv(g):
                wait(pe, xT_set, g + 1)
                wait(pe, z_set["ln0"], g - 1)
                pe.matmul(u_ps, w1a[:], xT[:], start=True, stop=True)
                pe.matmul(v_ps, w1b[:], xT[:], start=True, stop=True).then_inc(uv_made, 1)

            def products(g, t, block_of_duo):
                if block_of_duo == 0:
                    wait(pe, h_dve, SLOTS * g + t + 1)
                    wait(pe, h_act, SLOTS * g + t + 1)
                wait(pe, sq_done, 2 * (SLOTS * g + t) + block_of_duo - 3)
                c0 = block_of_duo * COLS
                pe.matmul(y_ps[:, t % 2, c0:c0 + COLS], w2c[:], h[:, t, c0:c0 + COLS], start=True, stop=True
                          ).then_inc(y_done, 1)

            def variances(g, t):
                half, p = t // HALF, (t % HALF) // 2
                wait(pe, sq_done, 2 * (SLOTS * g + t + 2))
                if p == 0:
                    wait(pe, dev_done, 2 * g + half)
                for q in range(4):
                    c0 = (q % 2) * COLS
                    mm = pe.matmul(ss_ps[32 * q:32 * q + 32, :], sel[:, ROWS - 1 - p:ROWS - 1 - p + 32],
                                   sq[:, (t + q // 2) % SQ_RING, c0:c0 + COLS],
                                   start=(p == 0), stop=(p == ROWS - 1))
                mm.then_inc(var_summed, 1)

            def broadcast(g, t, block_of_duo):
                half, p, q = t // HALF, (t % HALF) // 2, 2 * (t % 2) + block_of_duo
                if t % HALF == 0 and block_of_duo == 0:
                    wait(pe, c_rows_in[half], 48 * (g + 1))
                wait(pe, ttr_done, 2 * (SLOTS * g + t) + block_of_duo - 1)
                pe.matmul(cb_ps[:, block_of_duo, :], pick[:, 4 * q + p, :], c_rows[:, half, :],
                          start=True, stop=True).then_inc(bc_done, 1)

            def later_layers(g, lo, hi):
                def due(name):
                    return lo <= AT[name] < hi

                if g is None:
                    return
                if due("adj_turn"):
                    wait(pe, tail_in, 32 * (g + 1))
                    wait(pe, xT_set, min(g + 3, G) if isinstance(g, int) else g + 3)
                    pe.transpose(turn_ps, adj_in[:], ident[:]).then_inc(adj_turned, 1)
                if due("l0_mm"):
                    wait(pe, g_kept, g + 1)
                    wait(pe, adjT_set, g + 1)
                    pe.matmul(prod, gT_keep[:], w2cg[:], start=True, stop=False)
                    pe.matmul(prod, adjT[:], beta0[:], start=False, stop=True).then_inc(l0_made, 1)
                if due("l1_agg"):
                    wait(pe, x1s_set, g + 1)
                    wait(pe, uv_ready, min(g + 3, G) if isinstance(g, int) else g + 3)
                    wait(pe, z_set["ln0"], g + 1)
                    pe.matmul(prod, x1s[:], adjT[:], start=True, stop=True).then_inc(l1_agged, 1)
                if due("l1_mm"):
                    wait(pe, l1_agg_kept, g + 1)
                    pe.matmul(prod, aggT[:], l1wT[:], start=True, stop=True).then_inc(l1_made, 1)
                if due("l2_agg"):
                    wait(pe, normed["ln1"], g + 1)
                    wait(pe, adj_self_set, g + 1)
                    pe.matmul(prod, x2[:], adj_self[:], start=True, stop=True).then_inc(l2_agged, 1)
                if due("l2_mm1"):
                    wait(pe, l2_agg_kept, g + 1)
                    pe.matmul(prod, l2w1[:], aggT[:], start=True, stop=True).then_inc(l2_made1, 1)
                if due("l2_mm2"):
                    wait(pe, l2_relued, g + 1)
                    pe.matmul(prod, hid2[:], l2w2[:], start=True, stop=True).then_inc(l2_made2, 1)
                for i in range(LAYERS):
                    if due(f"l3_agg{i}"):
                        if i == 0:
                            wait(pe, normed["ln2"], g + 1)
                            wait(pe, adj_m_set, g + 1)
                        else:
                            wait(pe, l3_relued[i - 1], g + 1)
                        pe.matmul(prod, (x3 if i == 0 else h3)[:], adj_m[:], start=True, stop=True
                                  ).then_inc(l3_agged[i], 1)
                    if due(f"l3_mm{i}"):
                        wait(pe, l3_agg_kept[i], g + 1)
                        pe.matmul(prod, aggT[:], l3w[:, i, :], start=True, stop=True).then_inc(l3_made[i], 1)

            pe.wait_ge(ident_set, 1)
            pe.wait_ge(weights_in, WEIGHT_LOADS)
            pe.transpose(prod, l1w[:], ident[:]).then_inc(wT_turned, 1)
            pe.wait_ge(mask_cast, 1)
            pe.wait_ge(wT_set, 1)
            pe.transpose(turn_ps[:, 0:G], mask_f[:], ident[0:G, 0:G]).then_inc(mask_turned, 1)
            pe.wait_ge(mask_set, 1)
            turn_x(0)
            make_uv(0)
            pe.wait_ge(w2c_set, 1)
            pe.wait_ge(affine_set, 2)
            pe.wait_ge(ones_set, 3)
            pe.wait_ge(set_up, 1)

            def iteration(new, after, old, older):
                for s in range(SLOTS):
                    g, place0 = tail_graph(s, old, older)
                    yg, t = (new, s - 1) if s >= 1 else (old, SLOTS - 1)
                    wg, wt = (new, s - LAG) if s >= LAG else (old, s + SLOTS - LAG)
                    if s == SLOTS - 1 and after is not None:
                        make_uv(after)
                    if wg is not None:
                        broadcast(wg, wt, 0)
                    if yg is not None:
                        products(yg, t, 0)
                    if wg is not None:
                        broadcast(wg, wt, 1)
                    if s == 9 and after is not None:
                        turn_x(after)
                    later_layers(g, place0, place0 + FINE // 2)
                    if yg is not None:
                        products(yg, t, 1)
                    later_layers(g, place0 + FINE // 2, place0 + FINE)
                    sg, t = (new, s - 3) if s >= 3 else (old, s + SLOTS - 3)
                    if s % 2 == 1 and sg is not None:
                        variances(sg, t)

            program(pe, iteration)

        @block.scalar
        def _(act):
            def keep_xT(g):
                wait(act, x_turned, g + 1)
                wait(act, uv_made, g)
                act.activation(xT[:], turn_ps, ACT.Copy).then_inc(xT_set, 1)

            def keep_uv(g):
                wait(act, uv_made, g + 1)
                wait(act, pre_made, SLOTS * g)
                wait(act, h_dve, SLOTS * g)
                act.activation(uT[:], u_ps, ACT.Identity, bias=b1_col[:])
                act.activation(vT[:], v_ps, ACT.Copy).then_inc(uv_ready, 1)

            def hidden(g, t):
                wait(act, pre_made, SLOTS * g + t + 1)
                wait(act, ttr_done, 2 * (SLOTS * g + t - SLOTS + 1))
                act.activation(h[:, t, DVE_UNITS * P:], pre[:, t % PRE_RING, :], ACT.Relu).then_inc(h_act, 1)

            def squares(g, t, block_of_duo):
                wait(act, y_done, 2 * (SLOTS * g + t) + block_of_duo + 1)
                if block_of_duo == 0:
                    wait(act, var_summed, SLOTS // 2 * g + (t - SQ_RING) // 2 + 1)
                c0 = block_of_duo * COLS
                act.activation(sq[:, t % SQ_RING, c0:c0 + COLS], y_ps[:, t % 2, c0:c0 + COLS], ACT.Square,
                               bias=b2c_col[:], scale=float(P) ** -0.5).then_inc(sq_done, 1)

            def deviations(g, half):
                wait(act, var_summed, SLOTS // 2 * g + HALF // 2 * (half + 1))
                wait(act, dev_nat_in[half], 64 * g)
                act.activation(dev_rows[:, half, :], ss_ps[:], ACT.Sqrt, bias=EPS).then_inc(dev_done, 1)

            def later_layers(g, lo, hi):
                def due(name):
                    return lo <= AT[name] < hi

                if g is None:
                    return
                for name in NORMS:
                    if lo <= AT[name] + DEV_AT < hi:
                        wait(act, mv_set[name], g + 1)
                        act.activation(dev[:], mv[:, 1:2], ACT.Sqrt, bias=EPS).then_inc(dev_set[name], 1)
                if due("degree_root"):
                    wait(act, degree_set, g + 1)
                    wait(act, dis_raw_set, g)
                    act.activation(degree_root[:], degree[:], ACT.Sqrt).then_inc(degree_root_set, 1)
                if due("adj_turned"):
                    wait(act, adj_turned, g + 1)
                    wait(act, l1_agged, g)
                    act.activation(adjT[:], turn_ps, ACT.Copy).then_inc(adjT_set, 1)
                if due("l1_agg_keep"):
                    wait(act, l1_agged, g + 1)
                    wait(act, l3_made[LAYERS - 1], g)
                    act.activation(aggT[:], prod, ACT.Copy).then_inc(l1_agg_kept, 1)
                if due("l2_agg_keep"):
                    wait(act, l2_agged, g + 1)
                    act.activation(aggT[:], prod, ACT.Copy).then_inc(l2_agg_kept, 1)
                if due("l2_relu"):
                    wait(act, l2_made1, g + 1)
                    wait(act, l2_made2, g)
                    act.activation(hid2[:], prod, ACT.Relu, bias=l2b1[:]).then_inc(l2_relued, 1)
                for i in range(LAYERS):
                    if due(f"l3_agg_keep{i}"):
                        wait(act, l3_agged[i], g + 1)
                        act.activation(aggT[:], prod, ACT.Copy).then_inc(l3_agg_kept[i], 1)
                    if due(f"l3_relu{i}"):
                        wait(act, l3_affined[i], g + 1)
                        if i == 0:
                            wait(act, z_set["ln3"], g)
                        else:
                            wait(act, l3_based[i], g + 1)
                        act.activation(h3[:], z_aff[:], ACT.Relu).then_inc(l3_relued[i], 1)

            act.wait_ge(weights_in, WEIGHT_LOADS)
            act.wait_ge(wT_turned, 1)
            act.activation(l1wT[:], prod, ACT.Copy).then_inc(wT_set, 1)
            act.wait_ge(mask_turned, 1)
            act.activation(mask_all[:], turn_ps[:, 0:G], ACT.Copy).then_inc(mask_set, 1)
            keep_xT(0)
            keep_uv(0)
            act.wait_ge(b2c_set, 1)

            def iteration(new, after, old, older):
                for s in range(SLOTS):
                    if s == 2 and old is not None:
                        deviations(old, 1)
                    if s == 10 and new is not None:
                        deviations(new, 0)
                    g, place0 = tail_graph(s, old, older)
                    sg, t = (new, s - 2) if s >= 2 else (old, s + SLOTS - 2)
                    if sg is not None:
                        squares(sg, t, 1)
                    later_layers(g, place0, place0 + FINE // 3)
                    if new is not None:
                        hidden(new, s)
                    if s == 10 and after is not None:
                        keep_xT(after)
                    if s == SLOTS - 1 and after is not None:
                        keep_uv(after)
                    later_layers(g, place0 + FINE // 3, place0 + 2 * FINE // 3)
                    sg, t = (new, s - 1) if s >= 1 else (old, SLOTS - 1)
                    if sg is not None:
                        squares(sg, t, 0)
                    later_layers(g, place0 + 2 * FINE // 3, place0 + FINE)

            program(act, iteration)

        @block.vector
        def _(dve):
            def hidden(g, t, n):
                if n == 0:
                    if t == 0:
                        wait(dve, uv_ready, g + 1)
                    wait(dve, ttr_done, 2 * (SLOTS * g + t - SLOTS + 1))
                i = unit_of(t, n)
                op = dve.tensor_scalar(h[:, t, n * P:(n + 1) * P], vT[:], uT[:, i:i + 1], 0.0, ALU.add, ALU.max)
                if n == DVE_UNITS - 1:
                    op.then_inc(h_dve, 1)

            def weighted_sum(g, t, n):
                block_of_duo, k = n // BLOCK_UNITS, n % BLOCK_UNITS
                if k == 0:
                    wait(dve, bc_done, 2 * (SLOTS * g + t) + block_of_duo + 1)
                    if t == 0 and n == 0:
                        wait(dve, g_kept, g)
                i = unit_of(t, n)
                cols = slice(n * P, (n + 1) * P)
                op = dve.tensor_tensor_reduce(h[:, t, cols], h[:, t, cols], cb_ps[:, block_of_duo, k * P:(k + 1) * P], 1.0, 0.0,
                                              ALU.mult, ALU.add, gT[:, i:i + 1])
                if k == BLOCK_UNITS - 1:
                    op.then_inc(ttr_done, 1)

            def invert(g, half):
                rows = slice(64 * half, 64 * half + 64)
                wait(dve, dev_nat_in[half], 64 * (g + 1))
                wait(dve, part_done[0], 2 * g)
                dve.reciprocal(inv_nat[rows, :], dev_nat[rows, :]).then_inc(inv_done, 1)

            def sum_coefficients(g):
                wait(dve, c_made, 2 * (g + 1))
                wait(dve, x_bias_set, g)
                dve.tensor_reduce(c_sum[:], c_nat[:], AX.X, ALU.add).then_inc(c_sum_set, 1)

            def norm_steps(g, name, lo, hi):
                at = AT[name]
                if lo <= at < hi:
                    wait(dve, z_set[name], g + 1)
                    dve.bn_stats(stats[:], z[:]).then_inc(stats_set[name], 1)
                if lo <= at + 1 < hi:
                    wait_apart(dve, stats_set[name], g + 1)
                    dve.bn_aggr(mv[:], stats[:]).then_inc(mv_set[name], 1)
                if lo <= at + INV_AT < hi:
                    wait(dve, dev_set[name], g + 1)
                    dve.reciprocal(rs[:], dev[:]).then_inc(rs_set[name], 1)

            def norm(g, name, dst, lo, hi):
                norm_steps(g, name, lo, hi)
                if lo <= AT[name] + INV_AT + 1 < hi:
                    wait(dve, rs_set[name], g + 1)
                    dve.tensor_scalar(dst[:], z[:], mv[:, 0:1], rs[:], ALU.subtract, ALU.mult
                                      ).then_inc(normed[name], 1)

            def later_layers(g, lo, hi):
                def due(name):
                    return lo <= AT[name] < hi

                if g is None:
                    return
                if due("row_sum"):
                    wait(dve, tail_in, 32 * (g + 1))
                    dve.tensor_reduce(degree[:], adj_in[:], AX.X, ALU.add).then_inc(degree_set, 1)
                if due("degree"):
                    wait(dve, degree_set, g + 1)
                    dve.tensor_scalar(degree_ok[:], degree[:], 0.0, None, ALU.is_gt).then_inc(degree_ok_set, 1)
                if due("inv_degree"):
                    wait(dve, degree_root_set, g + 1)
                    dve.tensor_scalar(degree_root[:], degree_root[:], 1e-38, None, ALU.max).then_inc(degree_floor_set, 1)
                if due("inv_degree2"):
                    wait(dve, degree_floor_set, g + 1)
                    dve.reciprocal(dis_raw[:], degree_root[:]).then_inc(dis_raw_set, 1)
                if due("has_degree"):
                    wait(dve, degree_ok_set, g + 1)
                    wait(dve, dis_raw_set, g + 1)
                    wait(dve, x1s_set, g)
                    dve.tensor_tensor(dis[:], dis_raw[:], degree_ok[:], ALU.mult).then_inc(dis_set, 1)
                if due("g_keep"):
                    wait(dve, ttr_done, 2 * SLOTS * (g + 1))
                    wait(dve, l0_made, g)
                    dve.tensor_copy(gT_keep[:], gT[:]).then_inc(g_kept, 1)
                if due("l0_sum"):
                    wait(dve, l0_made, g + 1)
                    wait(dve, x_base_set, g + 1)
                    dve.tensor_tensor(z[:], prod, x_base[:], ALU.add).then_inc(z_set["ln0"], 1)
                norm(g, "ln0", x1, lo, hi)
                if due("l1_bias"):
                    wait(dve, l1_made, g + 1)
                    dve.scalar_tensor_tensor(out=z_aff[:], in0=prod, scalar=dis[:], in1=l1b[:],
                                             op0=ALU.mult, op1=ALU.add).then_inc(l1_biased, 1)
                if due("l1_relu"):
                    wait(dve, l1_biased, g + 1)
                    dve.scalar_tensor_tensor(out=z[:], in0=z_aff[:], scalar=0.0, in1=x1[:],
                                             op0=ALU.max, op1=ALU.add).then_inc(z_set["ln1"], 1)
                norm(g, "ln1", x2, lo, hi)
                if due("l2_sum"):
                    wait(dve, l2_made2, g + 1)
                    wait(dve, x2_base_set, g + 1)
                    dve.scalar_tensor_tensor(out=z[:], in0=prod, scalar=mask_col[:], in1=x2_base[:],
                                             op0=ALU.mult, op1=ALU.add).then_inc(z_set["ln2"], 1)
                norm(g, "ln2", x3, lo, hi)
                for i in range(LAYERS):
                    name = f"l3_ln{i}"
                    if due(f"l3_sum{i}"):
                        wait(dve, l3_made[i], g + 1)
                        wait(dve, l3_based[i], g + 1)
                        dve.tensor_tensor(z[:], prod, h3_base[:], ALU.add).then_inc(z_set[name], 1)
                    norm_steps(g, name, lo, hi)
                    if lo <= AT[name] + 2 < hi:
                        wait(dve, mv_set[name], g + 1)
                        if i > 0:
                            wait(dve, l3_relued[i - 1], g + 1)
                        else:
                            wait(dve, z_set["ln1"], g + 1)
                        dve.scalar_tensor_tensor(out=z_aff[:], in0=z[:], scalar=mv[:, 0:1], in1=l3g[:, i, :],
                                                 op0=ALU.subtract, op1=ALU.mult).then_inc(l3_scaled[i], 1)
                    if lo <= AT[name] + INV_AT + 1 < hi:
                        wait(dve, l3_scaled[i], g + 1)
                        wait(dve, rs_set[name], g + 1)
                        dve.scalar_tensor_tensor(out=z_aff[:], in0=z_aff[:], scalar=rs[:], in1=l3beta[:, i, :],
                                                 op0=ALU.mult, op1=ALU.add).then_inc(l3_affined[i], 1)
                if due("final_sum"):
                    wait(dve, l3_relued[LAYERS - 1], g + 1)
                    dve.tensor_tensor(z[:], h3[:], x3[:], ALU.add).then_inc(z_set["ln3"], 1)
                if lo <= AT["ln3"] + INV_AT + 1 < hi:
                    wait(dve, out_stored, 16 * g)
                norm(g, "ln3", x4, lo, hi)

            dve.wait_ge(weights_in, WEIGHT_LOADS)
            dve.tensor_reduce(w2_mean[:], w2[:], AX.X, ALU.add).then_inc(w2_meaned, 1)
            dve.tensor_reduce(b2_mean[:], b2_row[:], AX.X, ALU.add).then_inc(b2_meaned, 1)
            dve.wait_ge(w2_meaned, 1)
            dve.tensor_scalar(w2_mean[:], w2_mean[:], 1.0 / P, None, ALU.mult).then_inc(w2_meaned, 1)
            dve.wait_ge(b2_meaned, 1)
            dve.tensor_scalar(b2_mean[:], b2_mean[:], 1.0 / P, None, ALU.mult).then_inc(b2_meaned, 1)
            dve.wait_ge(w2_meaned, 2)
            dve.tensor_scalar(w2c[:], w2[:], w2_mean[:], None, ALU.subtract).then_inc(w2c_set, 1)
            dve.wait_ge(b2_meaned, 2)
            dve.tensor_scalar(b2c_col[:], b2_col[:], b2_mean[:], float(P) ** -0.5, ALU.subtract, ALU.mult
                              ).then_inc(b2c_set, 1)
            dve.wait_ge(w2c_set, 1)
            dve.tensor_tensor(w2cg[:], w2c[:], gamma0[:], ALU.mult).then_inc(affine_set, 1)
            dve.scalar_tensor_tensor(out=b2cg[:], in0=b2_row[:], scalar=b2_mean[:], in1=gamma0[:],
                                     op0=ALU.subtract, op1=ALU.mult).then_inc(affine_set, 1)
            dve.wait_ge(masks_in, 16)
            dve.tensor_copy(mask_f[:], mask_u8[:]).then_inc(mask_cast, 1)
            dve.tensor_scalar(l2eps[:], l2eps[:], 1.0, None, ALU.add).then_inc(eps_set, 1)
            dve.wait_ge(eps_set, 1)
            dve.wait_ge(ident_set, 1)
            dve.tensor_scalar(ident_eps[:], ident[:], l2eps[:], None, ALU.mult).then_inc(eps_set, 1)

            def iteration(new, after, old, older):
                for s in range(SLOTS):
                    g, place0 = tail_graph(s, old, older)
                    wg, t = (new, s - LAG) if s >= LAG else (old, s + SLOTS - LAG)
                    steps = DVE_UNITS + DUO_UNITS
                    for k in range(steps):
                        if k < DVE_UNITS and new is not None:
                            hidden(new, s, k)
                        if k >= DVE_UNITS and wg is not None:
                            weighted_sum(wg, t, k - DVE_UNITS)
                        later_layers(g, place0 + k * FINE // steps, place0 + (k + 1) * FINE // steps)
                        if k == INVERT_STEP and s == 3 and old is not None:
                            invert(old, 1)
                        if k == INVERT_STEP and s == 11 and new is not None:
                            invert(new, 0)
                    if s == 6 and old is not None:
                        sum_coefficients(old)

            program(dve, iteration)

        @block.gpsimd
        def _(pool):
            def prepare(g, t):
                if t == 0:
                    wait(pool, uv_ready, g + 1)
                wait(pool, h_act, SLOTS * g + t - PRE_RING + 1)
                for n, end in ((DVE_UNITS, BLOCK_UNITS), (BLOCK_UNITS, DUO_UNITS)):
                    units, i, c0 = end - n, unit_of(t, n), (n - DVE_UNITS) * P
                    op = pool.tensor_tensor(
                        pre[:, t % PRE_RING, c0:c0 + units * P].rearrange("p (i j) -> p i j", j=P),
                        vT[:].rearrange("p (o j) -> p o j", o=1).to_broadcast([P, units, P]),
                        uT[:, i:i + units].rearrange("p (i o) -> p i o", o=1).to_broadcast([P, units, P]), ALU.add)
                op.then_inc(pre_made, 1)

            def coefficients(g, half):
                n, rows = 2 * g + half, slice(0, 64 * (half + 1))
                wait(pool, inv_done, n + 1)
                wait(pool, adj_c_in, 16 * (g + 1))
                wait(pool, c_sum_set, g)
                wait(pool, rest_done, n)
                for i in range(2):
                    wait(pool, c_rows_in[i], 48 * (g if i >= half else g + 1))
                pool.tensor_tensor(c_nat[rows, :], adj_c[rows, :], inv_nat[rows, :], ALU.mult).then_inc(c_made, 1)
                pool.tensor_tensor(c_part[0][rows, :], adj_c[rows, :], inv_nat[rows, :], ALU.mult
                                   ).then_inc(part_done[0], 1)
                wait(pool, c_made, n + 1)
                wait(pool, part_done[0], n + 1)
                pool.tensor_tensor(c_part[1][rows, :], c_nat[rows, :], c_part[0][rows, :], ALU.subtract
                                   ).then_inc(part_done[1], 1)
                pool.tensor_tensor(c_rest[rows, :], c_nat[rows, :], c_part[0][rows, :], ALU.subtract
                                   ).then_inc(rest_done, 1)
                wait(pool, part_done[1], n + 1)
                wait(pool, rest_done, n + 1)
                pool.tensor_tensor(c_part[2][rows, :], c_rest[rows, :], c_part[1][rows, :], ALU.subtract
                                   ).then_inc(part_done[2], 1)

            def later_layers(g, lo, hi):
                def due(name):
                    return lo <= AT[name] < hi

                if g is None:
                    return
                if due("adj_loop"):
                    wait(pool, tail_in, 32 * (g + 1))
                    wait(pool, l2_agged, g)
                    pool.tensor_tensor(adj_self[:], adj_in[:], ident_eps[:], ALU.add).then_inc(adj_self_set, 1)
                if due("adj_keep"):
                    wait_apart(pool, l3_agged[LAYERS - 1], g)
                    pool.tensor_copy(adj_m[:], adj_in[:]).then_inc(adj_m_set, 1)
                    wait_apart(pool, x2_bias_set, g)
                    wait_apart(pool, z_set["ln2"], g)
                    pool.tensor_copy(mask_col[:], mask_all[:, g:g + 1] if isinstance(g, int)
                                     else mask_all[:, bass.ds(g, 1)]).then_inc(mask_col_set, 1)
                if due("x_bias"):
                    wait(pool, c_sum_set, g + 1)
                    pool.tensor_tensor(x_bias[:], b2cg[:], c_sum[:].to_broadcast([P, P]), ALU.mult
                                       ).then_inc(x_bias_set, 1)
                if due("x_base"):
                    wait(pool, x_bias_set, g + 1)
                    wait(pool, z_set["ln0"], g)
                    pool.tensor_tensor(x_base[:], x_bias[:], x_res[:], ALU.add).then_inc(x_base_set, 1)
                if due("x1_scaled"):
                    wait(pool, normed["ln0"], g + 1)
                    wait(pool, dis_set, g + 1)
                    pool.tensor_tensor(x1s[:], x1[:], dis[:].to_broadcast([P, P]), ALU.mult).then_inc(x1s_set, 1)
                if due("x2_bias"):
                    wait(pool, mask_col_set, g + 1)
                    pool.tensor_tensor(x2_bias[:], l2b2[:], mask_col[:].to_broadcast([P, P]), ALU.mult
                                       ).then_inc(x2_bias_set, 1)
                if due("x2_base"):
                    wait(pool, x2_bias_set, g + 1)
                    wait(pool, normed["ln1"], g + 1)
                    pool.tensor_tensor(x2_base[:], x2_bias[:], x2[:], ALU.add).then_inc(x2_base_set, 1)
                for i in range(LAYERS):
                    if due(f"l3_base{i}"):
                        wait(pool, normed["ln2"] if i == 0 else l3_relued[i - 1], g + 1)
                        if i > 0:
                            wait(pool, z_set[f"l3_ln{i - 1}"], g + 1)
                        pool.tensor_tensor(h3_base[:], (x3 if i == 0 else h3)[:], l3b[:, i, :], ALU.add
                                           ).then_inc(l3_based[i], 1)

            pool.memset(ident[:], 0.0).then_inc(ones_set, 1)
            pool.memset(sel[:], 0.0).then_inc(ones_set, 1)
            pool.wait_ge(ones_set, 2)
            pool.affine_select(out=ident[:], in_=ident[:], compare_op=ALU.not_equal, fill=1.0, base=0,
                               pattern=[[-1, P]], channel_multiplier=1).then_inc(ident_set, 1)
            pool.memset(sel[:, ROWS - 1:ROWS], 1.0).then_inc(ones_set, 1)
            pool.wait_ge(affine_set, 2)
            pool.wait_ge(eps_set, 2)
            pool.wait_ge(mask_set, 1)
            pool.memset(c_rows[:], 0.0)
            pool.wait_ge(ident_set, 1)
            for k in range(PARTS):
                rows = slice(32 * k, 32 * k + 32)
                op = pool.tensor_copy(pick[rows], ident[rows, 32 * k:32 * k + HALF_BLOCKS].rearrange(
                    "p (b o) -> p b o", o=1).to_broadcast([32, HALF_BLOCKS, P]))
                if k < PARTS - 1:
                    op.then_inc(pick_set, 1)
                    pool.wait_ge(pick_set, k + 1)
            op.then_inc(set_up, 1)

            pool.wait_ge(set_up, 1)
            prepare(0, 0)
            prepare(0, 1)

            def iteration(new, after, old, older):
                for s in range(SLOTS):
                    g, place0 = tail_graph(s, old, older)
                    if s == 12 and new is not None:
                        coefficients(new, 0)
                    if s == 4 and old is not None:
                        coefficients(old, 1)
                    later_layers(g, place0, place0 + FINE // 2)
                    if s + 2 < SLOTS and new is not None:
                        prepare(new, s + 2)
                    if s + 1 == SLOTS and after is not None:
                        prepare(after, 0)
                        prepare(after, 1)
                    later_layers(g, place0 + FINE // 2, place0 + FINE)

            program(pool, iteration)


_INS = ['x', 'adj', 'nodemask', 'L0_gnn_W1', 'L0_gnn_b1', 'L0_gnn_W2', 'L0_gnn_b2', 'L0_gnn_gamma', 'L0_gnn_beta',
        'L1_gnn_W', 'L1_gnn_b', 'L2_gnn_W1', 'L2_gnn_b1', 'L2_gnn_W2', 'L2_gnn_b2', 'L2_gnn_eps',
        'L3_gnn_Ws', 'L3_gnn_bs', 'L3_gnn_gammas', 'L3_gnn_betas']


def kernel(**inputs):
    import numpy as np
    import concourse.bacc as bacc
    from concourse.bass_utils import run_bass_kernel_spmd

    nc = bacc.Bacc("TRN2", target_bir_lowering=False, num_devices=1)
    arrays, args = {}, []
    for name in _INS:
        a = np.ascontiguousarray(inputs[name])
        arrays[f"in_{name}_dram"] = a
        args.append(nc.dram_tensor(f"in_{name}_dram", a.shape, mybir.dt.from_np(a.dtype), kind="ExternalInput").ap())
    shape = tuple(inputs["x"].shape)
    args.append(nc.dram_tensor("out_dram", shape, F32, kind="ExternalOutput").ap())
    build(nc, *args)
    r = run_bass_kernel_spmd(nc, [arrays], core_ids=[0])
    return r.results[0]["out_dram"]
```

```python
from contextlib import ExitStack

import concourse.bass as bass
from concourse import mybir

F32 = mybir.dt.float32
BF16 = mybir.dt.bfloat16
U8 = mybir.dt.uint8
ALU = mybir.AluOpType
ACT = mybir.ActivationFunctionType
AX = mybir.AxisListType

P = 128
EPS = 1e-5
BLOCK_UNITS = 4
COLS = BLOCK_UNITS * P
DUO_UNITS = 2 * BLOCK_UNITS
SLOTS = P // DUO_UNITS
HALF = SLOTS // 2
ROWS = HALF // 2
LAG = 14
LAYERS = 3
SQ_RING = 4
SPAN = P // 2
WEIGHTS = 7
LATER_WEIGHTS = 8 + 4 * LAYERS
PARTS = 3
HALF_BLOCKS = 2 * HALF
DVE_UNITS = 1
POOL_UNITS = DUO_UNITS - DVE_UNITS
PRE_RING = 4

FINE = 12
TAIL_SLOT = 12
DEV_AT, INV_AT = 4, 6
LATER_SET_UP_SLOT = 2
INVERT_STEP = 7


def unit_of(t, n):
    half, b = t // HALF, 2 * (t % HALF) + n // BLOCK_UNITS
    return 64 * half + 16 * (b % 4) + 4 * (b // 4) + n % BLOCK_UNITS


AT = {}


def place(name, slot, fine):
    AT[name] = slot * FINE + fine


for _name, _slot, _fine in [
    ("adj_turn", 0, 0), ("adj_turned", 0, 7), ("adj_loop", 0, 5), ("adj_keep", 2, 0), ("row_sum", 0, 2),
    ("degree", 0, 5), ("degree_root", 0, 7), ("inv_degree", 1, 0), ("has_degree", 1, 1),
    ("beta_degree", 0, 8), ("c_sum", 0, 1), ("x_bias", 0, 10), ("x_sum", 1, 3), ("x_base", 1, 3),
    ("g_keep", 1, 11), ("l0_mm", 2, 2), ("l0_sum", 2, 7), ("ln0", 2, 8), ("x1_scaled", 3, 4),
    ("l1_agg", 4, 4), ("l1_agg_keep", 4, 6), ("l1_mm", 4, 6), ("l1_bias", 4, 10), ("l1_relu", 5, 1),
    ("ln1", 5, 4), ("x2_bias", 4, 11), ("x2_base", 5, 3), ("l2_agg", 6, 1), ("l2_agg_keep", 6, 2),
    ("l2_mm1", 6, 6), ("l2_relu", 6, 6), ("l2_mm2", 7, 2), ("l2_sum", 7, 5), ("ln2", 7, 5),
    ("l3_base0", 8, 4), ("l3_agg0", 8, 2), ("l3_agg_keep0", 8, 5), ("l3_mm0", 8, 9), ("l3_sum0", 9, 2),
    ("l3_ln0", 9, 5), ("l3_relu0", 10, 1), ("l3_base1", 11, 4), ("l3_agg1", 10, 5), ("l3_agg_keep1", 11, 2),
    ("l3_mm1", 11, 0), ("l3_sum1", 11, 5), ("l3_ln1", 11, 5), ("l3_relu1", 12, 3), ("l3_base2", 12, 9),
    ("l3_agg2", 12, 3), ("l3_agg_keep2", 12, 7), ("l3_mm2", 12, 8), ("l3_sum2", 13, 5), ("l3_ln2", 13, 6),
    ("l3_relu2", 14, 3), ("final_sum", 14, 6), ("ln3", 14, 6),
]:
    place(_name, _slot, _fine)


def build(nc, x, adj, nodemask, l0_W1, l0_b1, l0_W2, l0_b2, l0_gamma, l0_beta, l1_W, l1_b,
          l2_W1, l2_b1, l2_W2, l2_b2, l2_eps, l3_Ws, l3_bs, l3_gammas, l3_betas, out):
    G = x.shape[0]
    assert x.shape[1] == x.shape[2] == adj.shape[1] == P

    with ExitStack() as ctx:
        def sb(name, shape, dt=F32):
            return ctx.enter_context(nc.sbuf_tensor(name, shape, dt))

        def ps(name, shape):
            return ctx.enter_context(nc.psum_tensor(name, shape, F32))

        def sem(name):
            return ctx.enter_context(nc.semaphore(name))

        ident = sb("ident", [P, P])
        ident_eps = sb("ident_eps", [P, P])
        sel = sb("sel", [P, 32 + ROWS - 1])
        w1a, w1b = sb("w1a", [P, P]), sb("w1b", [P, P])
        b1_col = sb("b1_col", [P, 1])
        w2 = sb("w2", [P, P])
        w2_mean = sb("w2_mean", [P, 1])
        w2c, w2cg = sb("w2c", [P, P]), sb("w2cg", [P, P])
        b2_row, b2_col = sb("b2_row", [P, P]), sb("b2_col", [P, 1])
        b2_mean = sb("b2_mean", [P, 1])
        b2c_col = sb("b2c_col", [P, 1])
        gamma0, beta0 = sb("gamma0", [P, P]), sb("beta0", [P, P])
        b2cg = sb("b2cg", [P, P])
        l1w, l1wT, l1b = sb("l1w", [P, P]), sb("l1wT", [P, P]), sb("l1b", [P, P])
        l2w1, l2w2 = sb("l2w1", [P, P]), sb("l2w2", [P, P])
        l2b1 = sb("l2b1", [P, 1])
        l2b2 = sb("l2b2", [P, P])
        l2eps = sb("l2eps", [P, 1])
        l3w = sb("l3w", [P, LAYERS, P])
        l3b, l3g, l3beta = sb("l3b", [P, LAYERS, P]), sb("l3g", [P, LAYERS, P]), sb("l3beta", [P, LAYERS, P])
        mask_u8, mask_f = sb("mask_u8", [G, P], U8), sb("mask_f", [G, P])
        mask_all = sb("mask_all", [P, G])

        x_in, xT = sb("x_in", [P, P]), sb("xT", [P, P])
        uT, vT = sb("uT", [P, P]), sb("vT", [P, P])
        h = sb("h", [P, SLOTS, DUO_UNITS * P])
        pre = sb("pre", [P, PRE_RING, POOL_UNITS * P])
        sq = sb("sq", [P, SQ_RING, DUO_UNITS * P])
        dev_rows = sb("dev_rows", [P, 2, COLS])
        devs, invs = sb("devs", [P, 2, SPAN]), sb("invs", [P, 2, SPAN])
        adj_c, c = sb("adj_c", [P, 2, SPAN]), sb("c", [P, 2, SPAN])
        c_rest = sb("c_rest", [P, 2, SPAN])
        c_part = [sb(f"c_part{k}", [P, 2, SPAN], BF16) for k in range(PARTS)]
        c_row_sum = sb("c_row_sum", [P, 2])
        c_pair = sb("c_pair", [P, 2])
        c_rows = sb("c_rows", [32 * PARTS, 2, COLS], BF16)
        pick = sb("pick", [32 * PARTS, HALF_BLOCKS, P], BF16)
        gT, gT_keep = sb("gT", [P, P]), sb("gT_keep", [P, P])

        adj_in, x_res = sb("adj_in", [P, P]), sb("x_res", [P, P])
        adjT, adj_self, adj_m = sb("adjT", [P, P]), sb("adj_self", [P, P]), sb("adj_m", [P, P])
        degree, degree_ok, dis = sb("degree", [P, 1]), sb("degree_ok", [P, 1]), sb("dis", [P, 1])
        degree_floor, degree_root = sb("degree_floor", [P, 1]), sb("degree_root", [P, 1])
        dis_raw = sb("dis_raw", [P, 1])
        c_sum = sb("c_sum", [P, 1])
        mask_col = sb("mask_col", [P, 1])
        x_bias, x_base = sb("x_bias_t", [P, P]), sb("x_base_t", [P, P])
        beta_degree, x_sum = sb("beta_degree_t", [P, P]), sb("x_sum_t", [P, P])
        x2_bias, x2_base = sb("x2_bias_t", [P, P]), sb("x2_base_t", [P, P])
        z = sb("z", [P, P])
        z_aff = sb("z_aff", [P, P])
        stats, mv, dev, rs = sb("stats", [P, 6]), sb("mv", [P, 2]), sb("dev", [P, 1]), sb("rs", [P, 1])
        x1, x1s, x2, x3 = sb("x1", [P, P]), sb("x1s", [P, P]), sb("x2", [P, P]), sb("x3", [P, P])
        aggT = sb("aggT", [P, P])
        hid2 = sb("hid2", [P, P])
        h3 = sb("h3", [P, P])
        h3_base = sb("h3_base", [P, P])
        x4 = sb("x4", [P, P])

        y_ps = ps("y_ps", [P, 2, DUO_UNITS * P])
        ss_ps = ps("ss_ps", [P, COLS])
        cb_ps = ps("cb_ps", [P, 2, COLS])
        small_ps = ps("small_ps", [P, 4, P])
        prod, turn_ps, u_ps, v_ps = (small_ps[:, i, :] for i in range(4))

        weights_in, later_weights_in, masks_in = sem("weights_in"), sem("later_weights_in"), sem("masks_in")
        ones_set, ident_set = sem("ones_set"), sem("ident_set")
        w2_meaned, w2c_set, b2_meaned, b2c_set, affine_set = (
            sem("w2_meaned"), sem("w2c_set"), sem("b2_meaned"), sem("b2c_set"), sem("affine_set"))
        mask_cast, mask_turned, mask_set = sem("mask_cast"), sem("mask_turned"), sem("mask_set")
        wT_turned, wT_set = sem("wT_turned"), sem("wT_set")
        eps_set = sem("eps_set")
        set_up, pick_set = sem("set_up"), sem("pick_set")
        x_in_in, x_turned, xT_set, uv_made, uv_ready = (
            sem("x_in_in"), sem("x_turned"), sem("xT_set"), sem("uv_made"), sem("uv_ready"))
        pre_made, h_dve, h_made = sem("pre_made"), sem("h_dve"), sem("h_made")
        y_done, sq_done = sem("y_done"), sem("sq_done")
        bc_done, ttr_done = sem("bc_done"), sem("ttr_done")
        var_summed = sem("var_summed")
        adj_c_in = sem("adj_c_in")
        devs_in = [sem(f"devs_in{i}") for i in range(2)]
        c_rows_in = [sem(f"c_rows_in{i}") for i in range(2)]
        dev_done, inv_done, c_made = sem("dev_done"), sem("inv_done"), sem("c_made")
        part_done = [sem(f"part_done{k}") for k in range(PARTS)]
        rest_done = sem("rest_done")
        tail_in, out_stored = sem("tail_in"), sem("out_stored")
        adj_turned, adjT_set, adj_self_set, adj_m_set = (
            sem("adj_turned"), sem("adjT_set"), sem("adj_self_set"), sem("adj_m_set"))
        degree_set, degree_ok_set, degree_root_set, dis_raw_set, dis_set, degree_floor_set = (
            sem("degree_set"), sem("degree_ok_set"), sem("degree_root_set"), sem("dis_raw_set"), sem("dis_set"),
            sem("degree_floor_set"))
        c_row_sum_set, c_pair_in, c_sum_set = sem("c_row_sum_set"), sem("c_pair_in"), sem("c_sum_set")
        x_bias_set, beta_degree_set, x_sum_set, x_base_set = (
            sem("x_bias_set"), sem("beta_degree_set"), sem("x_sum_set"), sem("x_base_set"))
        mask_col_set, x2_bias_set, x2_base_set = sem("mask_col_set"), sem("x2_bias_set"), sem("x2_base_set")
        g_kept, l0_made = sem("g_kept"), sem("l0_made")
        x1s_set, l1_agged, l1_agg_kept, l1_made, l1_biased = (
            sem("x1s_set"), sem("l1_agged"), sem("l1_agg_kept"), sem("l1_made"), sem("l1_biased"))
        l2_agged, l2_agg_kept, l2_made1, l2_relued, l2_made2 = (
            sem("l2_agged"), sem("l2_agg_kept"), sem("l2_made1"), sem("l2_relued"), sem("l2_made2"))
        l3_based = [sem(f"l3_based{i}") for i in range(LAYERS)]
        l3_agged = [sem(f"l3_agged{i}") for i in range(LAYERS)]
        l3_agg_kept = [sem(f"l3_agg_kept{i}") for i in range(LAYERS)]
        l3_made = [sem(f"l3_made{i}") for i in range(LAYERS)]
        l3_scaled = [sem(f"l3_scaled{i}") for i in range(LAYERS)]
        l3_affined = [sem(f"l3_affined{i}") for i in range(LAYERS)]
        l3_relued = [sem(f"l3_relued{i}") for i in range(LAYERS)]
        NORMS = ["ln0", "ln1", "ln2", "l3_ln0", "l3_ln1", "l3_ln2", "ln3"]
        z_set = {n: sem(f"z_set_{n}") for n in NORMS}
        stats_set = {n: sem(f"stats_set_{n}") for n in NORMS}
        mv_set = {n: sem(f"mv_set_{n}") for n in NORMS}
        dev_set = {n: sem(f"dev_set_{n}") for n in NORMS}
        rs_set = {n: sem(f"rs_set_{n}") for n in NORMS}
        normed = {n: sem(f"normed_{n}") for n in ("ln0", "ln1", "ln2", "ln3")}

        def wait(eng, s, value):
            if isinstance(value, int) and value <= 0:
                return
            eng.wait_ge(s, value)

        def wait_apart(eng, s, value):
            if not isinstance(value, int):
                eng.lower_val(value)
                eng.wait_ge(set_up, 1)
            wait(eng, s, value)

        def program(eng, iteration):
            iteration(new=0, after=1, old=None, older=None)
            iteration(new=1, after=2, old=0, older=None)
            iteration(new=2, after=3, old=1, older=0)
            with eng.Fori(3, G - 1) as g:
                iteration(new=g, after=g + 1, old=g - 1, older=g - 2)
            iteration(new=G - 1, after=None, old=G - 2, older=G - 3)
            iteration(new=None, after=None, old=G - 1, older=G - 2)
            iteration(new=None, after=None, old=None, older=G - 1)

        def is_graph(g, number):
            return isinstance(g, int) and g == number

        def tail_graph(s, old, older):
            if s >= TAIL_SLOT:
                return old, (s - TAIL_SLOT) * FINE
            return older, (s + SLOTS - TAIL_SLOT) * FINE

        block = ctx.enter_context(nc.Block())

        @block.sync
        def _(sp):
            def row(v):
                return v.partition_broadcast(P)

            def col(v):
                return v.rearrange("(p o) -> p o", o=1)

            def coefficient_rows(a):
                return a.rearrange("(h i) (l j) -> (i l) h j", h=2, l=2)

            sp.dma_start(x_in[:], x[0]).then_inc(x_in_in, 16)
            weights = [
                (w1a[:], l0_W1[0:P, :]), (w1b[:], l0_W1[P:2 * P, :]), (b1_col[:], col(l0_b1)),
                (w2[:], l0_W2), (b2_row[:], row(l0_b2)), (b2_col[:], col(l0_b2)), (gamma0[:], row(l0_gamma)),
            ]
            assert len(weights) == WEIGHTS
            for dst, src in weights:
                sp.dma_start(dst, src).then_inc(weights_in, 16)
            sp.wait_ge(set_up, 1)
            sp.dma_start(adj_c[:], coefficient_rows(adj[0])).then_inc(adj_c_in, 16)
            later_weights = [
                (beta0[:], row(l0_beta)), (l1w[:], l1_W), (l1b[:], row(l1_b)),
                (l2w1[:], l2_W1), (l2w2[:], l2_W2), (l2b1[:], col(l2_b1)), (l2b2[:], row(l2_b2)),
                (l2eps[:], row(l2_eps)),
            ]
            for i in range(LAYERS):
                later_weights += [(l3w[:, i, :], l3_Ws[i]), (l3b[:, i, :], row(l3_bs[i])),
                                  (l3g[:, i, :], row(l3_gammas[i])), (l3beta[:, i, :], row(l3_betas[i]))]
            assert len(later_weights) == LATER_WEIGHTS
            for dst, src in later_weights:
                sp.dma_start(dst, src).then_inc(later_weights_in, 16)
            sp.dma_start(mask_u8[:], nodemask).then_inc(masks_in, 16)

            def load_adj_c(g):
                wait_apart(sp, adj_c_in, 16 * g)
                sp.dma_start(adj_c[:], coefficient_rows(adj[g])).then_inc(adj_c_in, 16)

            def straighten_deviations(g, half):
                wait_apart(sp, dev_done, 2 * g + half + 1)
                wait_apart(sp, inv_done, 2 * (g - 1) + half + 1)
                wait_apart(sp, devs_in[half], 64 * g)
                for q in range(4):
                    sp.dma_start(devs[32 * q:32 * q + 32, half, :],
                                 dev_rows[32 * q:32 * q + ROWS, half, :].rearrange("p (r j) -> p r j", j=SPAN)
                                 ).then_inc(devs_in[half], 16)

            def line_up_coefficients(g, half):
                wait_apart(sp, bc_done, 2 * (SLOTS * g + HALF * (half - 1)))
                wait_apart(sp, c_rows_in[half], 48 * g)
                for k in range(PARTS):
                    wait_apart(sp, part_done[k], 2 * g + half + 1)
                    sp.dma_start(c_rows[32 * k:32 * k + HALF_BLOCKS, half, :].rearrange("b (r j) -> b r j", j=SPAN),
                                 c_part[k][:, half, :]).then_inc(c_rows_in[half], 16)

            def pair_sums(g):
                wait_apart(sp, c_row_sum_set, g + 1)
                wait_apart(sp, c_sum_set, g)
                wait_apart(sp, c_pair_in, 64 * g)
                for half in range(2):
                    for r in range(2):
                        sp.dma_start(c_pair[64 * half:64 * half + 64, r:r + 1], c_row_sum[r:P:2, half:half + 1]
                                     ).then_inc(c_pair_in, 16)

            def iteration(new, after, old, older):
                if after is not None:
                    wait_apart(sp, x_turned, new + 1)
                    wait_apart(sp, x_in_in, 16 * (new + 1))
                    sp.dma_start(x_in[:], x[after]).then_inc(x_in_in, 16)
                if old is not None:
                    straighten_deviations(old, 1)
                    line_up_coefficients(old, 1)
                    pair_sums(old)
                    if new is not None:
                        wait_apart(sp, part_done[0], 2 * (old + 1))
                        load_adj_c(new)
                    wait_apart(sp, adj_turned, old)
                    wait_apart(sp, adj_self_set, old)
                    wait_apart(sp, adj_m_set, old)
                    wait_apart(sp, degree_set, old)
                    wait_apart(sp, x_sum_set, old)
                    wait_apart(sp, tail_in, 32 * old)
                    sp.dma_start(adj_in[:], adj[old]).then_inc(tail_in, 16)
                    sp.dma_start(x_res[:], x[old]).then_inc(tail_in, 16)
                if new is not None:
                    straighten_deviations(new, 0)
                    line_up_coefficients(new, 0)
                if older is not None:
                    wait_apart(sp, normed["ln3"], older + 1)
                    wait_apart(sp, out_stored, 16 * older)
                    sp.dma_start(out[older], x4[:]).then_inc(out_stored, 16)

            program(sp, iteration)
            sp.wait_ge(out_stored, 16 * G)

        @block.tensor
        def _(pe):
            def turn_x(g):
                wait(pe, x_in_in, 16 * (g + 1))
                wait(pe, uv_ready, g)
                wait(pe, z_set["l3_ln2"], g - 2)
                pe.transpose(turn_ps, x_in[:], ident[:]).then_inc(x_turned, 1)

            def make_uv(g):
                wait(pe, xT_set, g + 1)
                wait(pe, z_set["ln0"], g - 1)
                pe.matmul(u_ps, w1a[:], xT[:], start=True, stop=True)
                pe.matmul(v_ps, w1b[:], xT[:], start=True, stop=True).then_inc(uv_made, 1)

            def products(g, t, block_of_duo):
                if block_of_duo == 0:
                    wait(pe, h_made, SLOTS * g + t + 1)
                    wait(pe, sq_done, 2 * (SLOTS * g + t - 1))
                c0 = block_of_duo * COLS
                pe.matmul(y_ps[:, t % 2, c0:c0 + COLS], w2c[:], h[:, t, c0:c0 + COLS], start=True, stop=True
                          ).then_inc(y_done, 1)

            def variances(g, t):
                half, p = t // HALF, (t % HALF) // 2
                wait(pe, sq_done, 2 * (SLOTS * g + t + 2))
                if p == 0:
                    wait(pe, dev_done, 2 * g + half)
                for q in range(4):
                    c0 = (q % 2) * COLS
                    mm = pe.matmul(ss_ps[32 * q:32 * q + 32, :], sel[:, ROWS - 1 - p:ROWS - 1 - p + 32],
                                   sq[:, (t + q // 2) % SQ_RING, c0:c0 + COLS],
                                   start=(p == 0), stop=(p == ROWS - 1))
                mm.then_inc(var_summed, 1)

            def broadcast(g, t, block_of_duo):
                half, p, q = t // HALF, (t % HALF) // 2, 2 * (t % 2) + block_of_duo
                if t % HALF == 0 and block_of_duo == 0:
                    wait(pe, c_rows_in[half], 48 * (g + 1))
                wait(pe, ttr_done, 2 * (SLOTS * g + t) + block_of_duo - 1)
                pe.matmul(cb_ps[:, block_of_duo, :], pick[:, 4 * q + p, :], c_rows[:, half, :],
                          start=True, stop=True).then_inc(bc_done, 1)

            def later_layers(g, lo, hi):
                def due(name):
                    return lo <= AT[name] < hi

                if g is None:
                    return
                if due("adj_turn"):
                    wait(pe, tail_in, 32 * (g + 1))
                    wait(pe, xT_set, min(g + 3, G) if isinstance(g, int) else g + 3)
                    pe.transpose(turn_ps, adj_in[:], ident[:]).then_inc(adj_turned, 1)
                if due("l0_mm"):
                    wait(pe, g_kept, g + 1)
                    wait(pe, adjT_set, g + 1)
                    pe.matmul(prod, gT_keep[:], w2cg[:], start=True, stop=True).then_inc(l0_made, 1)
                if due("l1_agg"):
                    wait(pe, x1s_set, g + 1)
                    wait(pe, uv_ready, min(g + 3, G) if isinstance(g, int) else g + 3)
                    wait(pe, z_set["ln0"], g + 1)
                    pe.matmul(prod, x1s[:], adjT[:], start=True, stop=True).then_inc(l1_agged, 1)
                if due("l1_mm"):
                    wait(pe, l1_agg_kept, g + 1)
                    pe.matmul(prod, aggT[:], l1wT[:], start=True, stop=True).then_inc(l1_made, 1)
                if due("l2_agg"):
                    wait(pe, normed["ln1"], g + 1)
                    wait(pe, adj_self_set, g + 1)
                    pe.matmul(prod, x2[:], adj_self[:], start=True, stop=True).then_inc(l2_agged, 1)
                if due("l2_mm1"):
                    wait(pe, l2_agg_kept, g + 1)
                    pe.matmul(prod, l2w1[:], aggT[:], start=True, stop=True).then_inc(l2_made1, 1)
                if due("l2_mm2"):
                    wait(pe, l2_relued, g + 1)
                    pe.matmul(prod, hid2[:], l2w2[:], start=True, stop=True).then_inc(l2_made2, 1)
                for i in range(LAYERS):
                    if due(f"l3_agg{i}"):
                        if i == 0:
                            wait(pe, normed["ln2"], g + 1)
                            wait(pe, adj_m_set, g + 1)
                        else:
                            wait(pe, l3_relued[i - 1], g + 1)
                        pe.matmul(prod, (x3 if i == 0 else h3)[:], adj_m[:], start=True, stop=True
                                  ).then_inc(l3_agged[i], 1)
                    if due(f"l3_mm{i}"):
                        wait(pe, l3_agg_kept[i], g + 1)
                        pe.matmul(prod, aggT[:], l3w[:, i, :], start=True, stop=True).then_inc(l3_made[i], 1)

            def later_set_up():
                pe.wait_ge(later_weights_in, 16 * LATER_WEIGHTS)
                pe.wait_ge(uv_ready, 2)
                pe.transpose(prod, l1w[:], ident[:]).then_inc(wT_turned, 1)
                pe.wait_ge(mask_cast, 1)
                pe.wait_ge(wT_set, 1)
                pe.transpose(turn_ps[:, 0:G], mask_f[:], ident[0:G, 0:G]).then_inc(mask_turned, 1)
                pe.wait_ge(mask_set, 1)

            pe.wait_ge(ident_set, 1)
            turn_x(0)
            pe.wait_ge(weights_in, 16 * WEIGHTS)
            make_uv(0)
            pe.wait_ge(w2c_set, 1)
            pe.wait_ge(affine_set, 2)
            pe.wait_ge(ones_set, 3)
            pe.wait_ge(set_up, 1)

            def iteration(new, after, old, older):
                for s in range(SLOTS):
                    if is_graph(new, 1) and s == LATER_SET_UP_SLOT:
                        later_set_up()
                    g, place0 = tail_graph(s, old, older)
                    yg, t = (new, s - 1) if s >= 1 else (old, SLOTS - 1)
                    wg, wt = (new, s - LAG) if s >= LAG else (old, s + SLOTS - LAG)
                    if s == SLOTS - 1 and after is not None:
                        make_uv(after)
                    if wg is not None:
                        broadcast(wg, wt, 0)
                    if yg is not None:
                        products(yg, t, 0)
                    if wg is not None:
                        broadcast(wg, wt, 1)
                    if s == 10 and after is not None:
                        turn_x(after)
                    later_layers(g, place0, place0 + FINE // 2)
                    if yg is not None:
                        products(yg, t, 1)
                    later_layers(g, place0 + FINE // 2, place0 + FINE)
                    sg, t = (new, s - 3) if s >= 3 else (old, s + SLOTS - 3)
                    if s % 2 == 1 and sg is not None:
                        variances(sg, t)

            program(pe, iteration)

        @block.scalar
        def _(act):
            def keep_xT(g):
                wait(act, x_turned, g + 1)
                wait(act, uv_made, g)
                act.activation(xT[:], turn_ps, ACT.Copy).then_inc(xT_set, 1)

            def keep_uv(g):
                wait(act, uv_made, g + 1)
                wait(act, pre_made, SLOTS * g)
                wait(act, h_dve, SLOTS * g)
                act.activation(uT[:], u_ps, ACT.Identity, bias=b1_col[:])
                act.activation(vT[:], v_ps, ACT.Copy).then_inc(uv_ready, 1)

            def hidden(g, t):
                wait(act, pre_made, SLOTS * g + t + 1)
                wait(act, h_dve, SLOTS * g + t + 1)
                act.activation(h[:, t, DVE_UNITS * P:], pre[:, t % PRE_RING, :], ACT.Relu).then_inc(h_made, 1)

            def squares(g, t, block_of_duo):
                wait(act, y_done, 2 * (SLOTS * g + t) + block_of_duo + 1)
                if block_of_duo == 0:
                    wait(act, var_summed, SLOTS // 2 * g + (t - SQ_RING) // 2 + 1)
                c0 = block_of_duo * COLS
                act.activation(sq[:, t % SQ_RING, c0:c0 + COLS], y_ps[:, t % 2, c0:c0 + COLS], ACT.Square,
                               bias=b2c_col[:], scale=float(P) ** -0.5).then_inc(sq_done, 1)

            def deviations(g, half):
                wait(act, var_summed, SLOTS // 2 * g + HALF // 2 * (half + 1))
                wait(act, devs_in[half], 64 * g)
                act.activation(dev_rows[:, half, :], ss_ps[:], ACT.Sqrt, bias=EPS).then_inc(dev_done, 1)

            def later_layers(g, lo, hi):
                def due(name):
                    return lo <= AT[name] < hi

                if g is None:
                    return
                for name in NORMS:
                    if lo <= AT[name] + DEV_AT < hi:
                        wait(act, mv_set[name], g + 1)
                        act.activation(dev[:], mv[:, 1:2], ACT.Sqrt, bias=EPS).then_inc(dev_set[name], 1)
                if due("beta_degree"):
                    wait(act, degree_set, g + 1)
                    wait(act, x_sum_set, g)
                    act.activation(beta_degree[:], beta0[:], ACT.Copy, scale=degree[:]).then_inc(beta_degree_set, 1)
                if due("degree_root"):
                    wait(act, degree_floor_set, g + 1)
                    wait(act, dis_raw_set, g)
                    act.activation(degree_root[:], degree_floor[:], ACT.Sqrt).then_inc(degree_root_set, 1)
                if due("adj_turned"):
                    wait(act, adj_turned, g + 1)
                    wait(act, l1_agged, g)
                    act.activation(adjT[:], turn_ps, ACT.Copy).then_inc(adjT_set, 1)
                if due("l1_agg_keep"):
                    wait(act, l1_agged, g + 1)
                    wait(act, l3_made[LAYERS - 1], g)
                    act.activation(aggT[:], prod, ACT.Copy).then_inc(l1_agg_kept, 1)
                if due("l2_agg_keep"):
                    wait(act, l2_agged, g + 1)
                    act.activation(aggT[:], prod, ACT.Copy).then_inc(l2_agg_kept, 1)
                if due("l2_relu"):
                    wait(act, l2_made1, g + 1)
                    wait(act, l2_made2, g)
                    act.activation(hid2[:], prod, ACT.Relu, bias=l2b1[:]).then_inc(l2_relued, 1)
                for i in range(LAYERS):
                    if due(f"l3_agg_keep{i}"):
                        wait(act, l3_agged[i], g + 1)
                        act.activation(aggT[:], prod, ACT.Copy).then_inc(l3_agg_kept[i], 1)
                    if due(f"l3_relu{i}"):
                        wait(act, l3_affined[i], g + 1)
                        if i == 0:
                            wait(act, z_set["ln3"], g)
                        else:
                            wait(act, l3_based[i], g + 1)
                        act.activation(h3[:], z_aff[:], ACT.Relu).then_inc(l3_relued[i], 1)

            def later_set_up():
                act.wait_ge(later_weights_in, 16 * LATER_WEIGHTS)
                act.wait_ge(wT_turned, 1)
                act.activation(l1wT[:], prod, ACT.Copy).then_inc(wT_set, 1)
                act.wait_ge(mask_turned, 1)
                act.activation(mask_all[:], turn_ps[:, 0:G], ACT.Copy).then_inc(mask_set, 1)

            act.wait_ge(weights_in, 16 * WEIGHTS)
            keep_xT(0)
            keep_uv(0)
            act.wait_ge(b2c_set, 1)

            def iteration(new, after, old, older):
                for s in range(SLOTS):
                    if is_graph(new, 1) and s == LATER_SET_UP_SLOT:
                        later_set_up()
                    if s == 2 and old is not None:
                        deviations(old, 1)
                    if s == 10 and new is not None:
                        deviations(new, 0)
                    g, place0 = tail_graph(s, old, older)
                    sg, t = (new, s - 2) if s >= 2 else (old, s + SLOTS - 2)
                    if sg is not None:
                        squares(sg, t, 1)
                    later_layers(g, place0, place0 + FINE // 3)
                    if new is not None:
                        hidden(new, s)
                    if s == 11 and after is not None:
                        keep_xT(after)
                    if s == SLOTS - 1 and after is not None:
                        keep_uv(after)
                    later_layers(g, place0 + FINE // 3, place0 + 2 * FINE // 3)
                    sg, t = (new, s - 1) if s >= 1 else (old, SLOTS - 1)
                    if sg is not None:
                        squares(sg, t, 0)
                    later_layers(g, place0 + 2 * FINE // 3, place0 + FINE)

            program(act, iteration)

        @block.vector
        def _(dve):
            def hidden(g, t, n):
                if n == 0 and t == 0:
                    wait(dve, uv_ready, g + 1)
                i = unit_of(t, n)
                op = dve.tensor_scalar(h[:, t, n * P:(n + 1) * P], vT[:], uT[:, i:i + 1], 0.0, ALU.add, ALU.max)
                if n == DVE_UNITS - 1:
                    op.then_inc(h_dve, 1)

            def weighted_sum(g, t, n):
                block_of_duo, k = n // BLOCK_UNITS, n % BLOCK_UNITS
                if k == 0:
                    wait(dve, bc_done, 2 * (SLOTS * g + t) + block_of_duo + 1)
                    if t == 0 and n == 0:
                        wait(dve, g_kept, g)
                i = unit_of(t, n)
                cols = slice(n * P, (n + 1) * P)
                op = dve.tensor_tensor_reduce(h[:, t, cols], h[:, t, cols], cb_ps[:, block_of_duo, k * P:(k + 1) * P],
                                              1.0, 0.0, ALU.mult, ALU.add, gT[:, i:i + 1])
                if k == BLOCK_UNITS - 1:
                    op.then_inc(ttr_done, 1)

            def invert(g, half):
                wait(dve, devs_in[half], 64 * (g + 1))
                wait(dve, part_done[0], 2 * (g - 1) + half + 1)
                dve.reciprocal(invs[:, half, :], devs[:, half, :]).then_inc(inv_done, 1)

            def sum_coefficients(g):
                wait(dve, c_made, 2 * (g + 1))
                wait(dve, c_pair_in, 64 * g)
                dve.tensor_reduce(c_row_sum[:], c[:], AX.X, ALU.add).then_inc(c_row_sum_set, 1)

            def norm_steps(g, name, lo, hi):
                at = AT[name]
                if lo <= at < hi:
                    wait(dve, z_set[name], g + 1)
                    dve.bn_stats(stats[:], z[:]).then_inc(stats_set[name], 1)
                if lo <= at + 1 < hi:
                    wait_apart(dve, stats_set[name], g + 1)
                    dve.bn_aggr(mv[:], stats[:]).then_inc(mv_set[name], 1)
                if lo <= at + INV_AT < hi:
                    wait(dve, dev_set[name], g + 1)
                    dve.reciprocal(rs[:], dev[:]).then_inc(rs_set[name], 1)

            def norm(g, name, dst, lo, hi):
                norm_steps(g, name, lo, hi)
                if lo <= AT[name] + INV_AT + 1 < hi:
                    wait(dve, rs_set[name], g + 1)
                    dve.tensor_scalar(dst[:], z[:], mv[:, 0:1], rs[:], ALU.subtract, ALU.mult
                                      ).then_inc(normed[name], 1)

            def later_layers(g, lo, hi):
                def due(name):
                    return lo <= AT[name] < hi

                if g is None:
                    return
                if due("row_sum"):
                    wait(dve, tail_in, 32 * (g + 1))
                    wait(dve, beta_degree_set, g)
                    dve.tensor_reduce(degree[:], adj_in[:], AX.X, ALU.add).then_inc(degree_set, 1)
                if due("degree"):
                    wait(dve, degree_set, g + 1)
                    dve.tensor_scalar(degree_ok[:], degree[:], 0.0, None, ALU.is_gt).then_inc(degree_ok_set, 1)
                    dve.tensor_scalar(degree_floor[:], degree[:], 1e-38, None, ALU.max).then_inc(degree_floor_set, 1)
                if due("inv_degree"):
                    wait(dve, degree_root_set, g + 1)
                    dve.reciprocal(dis_raw[:], degree_root[:]).then_inc(dis_raw_set, 1)
                if due("has_degree"):
                    wait(dve, degree_ok_set, g + 1)
                    wait(dve, dis_raw_set, g + 1)
                    wait(dve, x1s_set, g)
                    dve.tensor_tensor(dis[:], dis_raw[:], degree_ok[:], ALU.mult).then_inc(dis_set, 1)
                if due("g_keep"):
                    wait(dve, ttr_done, 2 * SLOTS * (g + 1))
                    wait(dve, l0_made, g)
                    dve.tensor_copy(gT_keep[:], gT[:]).then_inc(g_kept, 1)
                if due("l0_sum"):
                    wait(dve, l0_made, g + 1)
                    wait(dve, x_base_set, g + 1)
                    dve.tensor_tensor(z[:], prod, x_base[:], ALU.add).then_inc(z_set["ln0"], 1)
                norm(g, "ln0", x1, lo, hi)
                if due("l1_bias"):
                    wait(dve, l1_made, g + 1)
                    dve.scalar_tensor_tensor(out=z_aff[:], in0=prod, scalar=dis[:], in1=l1b[:],
                                             op0=ALU.mult, op1=ALU.add).then_inc(l1_biased, 1)
                if due("l1_relu"):
                    wait(dve, l1_biased, g + 1)
                    dve.scalar_tensor_tensor(out=z[:], in0=z_aff[:], scalar=0.0, in1=x1[:],
                                             op0=ALU.max, op1=ALU.add).then_inc(z_set["ln1"], 1)
                norm(g, "ln1", x2, lo, hi)
                if due("l2_sum"):
                    wait(dve, l2_made2, g + 1)
                    wait(dve, x2_base_set, g + 1)
                    dve.scalar_tensor_tensor(out=z[:], in0=prod, scalar=mask_col[:], in1=x2_base[:],
                                             op0=ALU.mult, op1=ALU.add).then_inc(z_set["ln2"], 1)
                norm(g, "ln2", x3, lo, hi)
                for i in range(LAYERS):
                    name = f"l3_ln{i}"
                    if due(f"l3_sum{i}"):
                        wait(dve, l3_made[i], g + 1)
                        wait(dve, l3_based[i], g + 1)
                        dve.tensor_tensor(z[:], prod, h3_base[:], ALU.add).then_inc(z_set[name], 1)
                    norm_steps(g, name, lo, hi)
                    if lo <= AT[name] + 2 < hi:
                        wait(dve, mv_set[name], g + 1)
                        if i > 0:
                            wait(dve, l3_relued[i - 1], g + 1)
                        else:
                            wait(dve, z_set["ln1"], g + 1)
                        dve.scalar_tensor_tensor(out=z_aff[:], in0=z[:], scalar=mv[:, 0:1], in1=l3g[:, i, :],
                                                 op0=ALU.subtract, op1=ALU.mult).then_inc(l3_scaled[i], 1)
                    if lo <= AT[name] + INV_AT + 1 < hi:
                        wait(dve, l3_scaled[i], g + 1)
                        wait(dve, rs_set[name], g + 1)
                        dve.scalar_tensor_tensor(out=z_aff[:], in0=z_aff[:], scalar=rs[:], in1=l3beta[:, i, :],
                                                 op0=ALU.mult, op1=ALU.add).then_inc(l3_affined[i], 1)
                if due("final_sum"):
                    wait(dve, l3_relued[LAYERS - 1], g + 1)
                    dve.tensor_tensor(z[:], h3[:], x3[:], ALU.add).then_inc(z_set["ln3"], 1)
                if lo <= AT["ln3"] + INV_AT + 1 < hi:
                    wait(dve, out_stored, 16 * g)
                norm(g, "ln3", x4, lo, hi)

            dve.wait_ge(ident_set, 1)
            for k in range(PARTS):
                rows = slice(32 * k, 32 * k + 32)
                if k == PARTS - 1:
                    dve.wait_ge(ones_set, 4)
                    dve.wait_ge(pick_set, k)
                dve.tensor_copy(pick[rows], ident[rows, 32 * k:32 * k + HALF_BLOCKS].rearrange(
                    "p (b o) -> p b o", o=1).to_broadcast([32, HALF_BLOCKS, P])
                    ).then_inc(set_up if k == PARTS - 1 else pick_set, 1)
            dve.wait_ge(weights_in, 16 * WEIGHTS)
            dve.tensor_reduce(w2_mean[:], w2[:], AX.X, ALU.add).then_inc(w2_meaned, 1)
            dve.tensor_reduce(b2_mean[:], b2_row[:], AX.X, ALU.add).then_inc(b2_meaned, 1)
            dve.wait_ge(w2_meaned, 1)
            dve.tensor_scalar(w2_mean[:], w2_mean[:], 1.0 / P, None, ALU.mult).then_inc(w2_meaned, 1)
            dve.wait_ge(b2_meaned, 1)
            dve.tensor_scalar(b2_mean[:], b2_mean[:], 1.0 / P, None, ALU.mult).then_inc(b2_meaned, 1)
            dve.wait_ge(w2_meaned, 2)
            dve.tensor_scalar(w2c[:], w2[:], w2_mean[:], None, ALU.subtract).then_inc(w2c_set, 1)
            dve.wait_ge(b2_meaned, 2)
            dve.tensor_scalar(b2c_col[:], b2_col[:], b2_mean[:], float(P) ** -0.5, ALU.subtract, ALU.mult
                              ).then_inc(b2c_set, 1)
            dve.wait_ge(w2c_set, 1)
            dve.tensor_tensor(w2cg[:], w2c[:], gamma0[:], ALU.mult).then_inc(affine_set, 1)
            dve.scalar_tensor_tensor(out=b2cg[:], in0=b2_row[:], scalar=b2_mean[:], in1=gamma0[:],
                                     op0=ALU.subtract, op1=ALU.mult).then_inc(affine_set, 1)

            def later_set_up():
                dve.wait_ge(masks_in, 16)
                dve.tensor_copy(mask_f[:], mask_u8[:]).then_inc(mask_cast, 1)
                dve.wait_ge(later_weights_in, 16 * LATER_WEIGHTS)
                dve.tensor_scalar(l2eps[:], l2eps[:], 1.0, None, ALU.add).then_inc(eps_set, 1)
                dve.wait_ge(eps_set, 1)
                dve.tensor_scalar(ident_eps[:], ident[:], l2eps[:], None, ALU.mult).then_inc(eps_set, 1)

            def iteration(new, after, old, older):
                for s in range(SLOTS):
                    if is_graph(new, 1) and s == LATER_SET_UP_SLOT - 1:
                        later_set_up()
                    g, place0 = tail_graph(s, old, older)
                    wg, t = (new, s - LAG) if s >= LAG else (old, s + SLOTS - LAG)
                    steps = DVE_UNITS + DUO_UNITS
                    for k in range(steps):
                        if k < DVE_UNITS and new is not None:
                            hidden(new, s, k)
                        if k >= DVE_UNITS and wg is not None:
                            weighted_sum(wg, t, k - DVE_UNITS)
                        later_layers(g, place0 + k * FINE // steps, place0 + (k + 1) * FINE // steps)
                        if k == INVERT_STEP and s == 3 and old is not None:
                            invert(old, 1)
                        if k == INVERT_STEP and s == 11 and new is not None:
                            invert(new, 0)
                    if s == 6 and old is not None:
                        sum_coefficients(old)

            program(dve, iteration)

        @block.gpsimd
        def _(pool):
            def prepare(g, t):
                if t == 0:
                    wait(pool, uv_ready, g + 1)
                wait(pool, h_made, SLOTS * g + t - PRE_RING + 1)
                for n, end in ((DVE_UNITS, BLOCK_UNITS), (BLOCK_UNITS, DUO_UNITS)):
                    units, i, c0 = end - n, unit_of(t, n), (n - DVE_UNITS) * P
                    op = pool.tensor_tensor(
                        pre[:, t % PRE_RING, c0:c0 + units * P].rearrange("p (i j) -> p i j", j=P),
                        vT[:].rearrange("p (o j) -> p o j", o=1).to_broadcast([P, units, P]),
                        uT[:, i:i + units].rearrange("p (i o) -> p i o", o=1).to_broadcast([P, units, P]), ALU.add)
                op.then_inc(pre_made, 1)

            def coefficients(g, half):
                n = 2 * g + half
                wait(pool, inv_done, n + 1)
                if half == 0:
                    wait(pool, adj_c_in, 16 * (g + 1))
                    wait(pool, c_row_sum_set, g)
                wait(pool, c_rows_in[half], 48 * g)
                pool.tensor_tensor(c[:, half, :], adj_c[:, half, :], invs[:, half, :], ALU.mult).then_inc(c_made, 1)
                pool.tensor_tensor(c_part[0][:, half, :], adj_c[:, half, :], invs[:, half, :], ALU.mult
                                   ).then_inc(part_done[0], 1)
                wait(pool, c_made, n + 1)
                wait(pool, part_done[0], n + 1)
                pool.tensor_tensor(c_part[1][:, half, :], c[:, half, :], c_part[0][:, half, :], ALU.subtract
                                   ).then_inc(part_done[1], 1)
                pool.tensor_tensor(c_rest[:, half, :], c[:, half, :], c_part[0][:, half, :], ALU.subtract
                                   ).then_inc(rest_done, 1)
                wait(pool, part_done[1], n + 1)
                wait(pool, rest_done, n + 1)
                pool.tensor_tensor(c_part[2][:, half, :], c_rest[:, half, :], c_part[1][:, half, :], ALU.subtract
                                   ).then_inc(part_done[2], 1)

            def later_layers(g, lo, hi):
                def due(name):
                    return lo <= AT[name] < hi

                if g is None:
                    return
                if due("adj_loop"):
                    wait(pool, tail_in, 32 * (g + 1))
                    wait(pool, l2_agged, g)
                    pool.tensor_tensor(adj_self[:], adj_in[:], ident_eps[:], ALU.add).then_inc(adj_self_set, 1)
                if due("adj_keep"):
                    wait_apart(pool, l3_agged[LAYERS - 1], g)
                    pool.tensor_copy(adj_m[:], adj_in[:]).then_inc(adj_m_set, 1)
                    wait_apart(pool, x2_bias_set, g)
                    wait_apart(pool, z_set["ln2"], g)
                    pool.tensor_copy(mask_col[:], mask_all[:, g:g + 1] if isinstance(g, int)
                                     else mask_all[:, bass.ds(g, 1)]).then_inc(mask_col_set, 1)
                if due("c_sum"):
                    wait(pool, c_pair_in, 64 * (g + 1))
                    wait(pool, x_bias_set, g)
                    pool.tensor_tensor(c_sum[:], c_pair[:, 0:1], c_pair[:, 1:2], ALU.add).then_inc(c_sum_set, 1)
                if due("x_bias"):
                    wait(pool, c_sum_set, g + 1)
                    pool.tensor_tensor(x_bias[:], b2cg[:], c_sum[:].to_broadcast([P, P]), ALU.mult
                                       ).then_inc(x_bias_set, 1)
                if due("x_sum"):
                    wait(pool, beta_degree_set, g + 1)
                    wait(pool, x_base_set, g)
                    pool.tensor_tensor(x_sum[:], beta_degree[:], x_res[:], ALU.add).then_inc(x_sum_set, 1)
                if due("x_base"):
                    wait(pool, x_sum_set, g + 1)
                    wait(pool, z_set["ln0"], g)
                    pool.tensor_tensor(x_base[:], x_bias[:], x_sum[:], ALU.add).then_inc(x_base_set, 1)
                if due("x1_scaled"):
                    wait(pool, normed["ln0"], g + 1)
                    wait(pool, dis_set, g + 1)
                    pool.tensor_tensor(x1s[:], x1[:], dis[:].to_broadcast([P, P]), ALU.mult).then_inc(x1s_set, 1)
                if due("x2_bias"):
                    wait(pool, mask_col_set, g + 1)
                    pool.tensor_tensor(x2_bias[:], l2b2[:], mask_col[:].to_broadcast([P, P]), ALU.mult
                                       ).then_inc(x2_bias_set, 1)
                if due("x2_base"):
                    wait(pool, x2_bias_set, g + 1)
                    wait(pool, normed["ln1"], g + 1)
                    pool.tensor_tensor(x2_base[:], x2_bias[:], x2[:], ALU.add).then_inc(x2_base_set, 1)
                for i in range(LAYERS):
                    if due(f"l3_base{i}"):
                        wait(pool, normed["ln2"] if i == 0 else l3_relued[i - 1], g + 1)
                        if i > 0:
                            wait(pool, z_set[f"l3_ln{i - 1}"], g + 1)
                        pool.tensor_tensor(h3_base[:], (x3 if i == 0 else h3)[:], l3b[:, i, :], ALU.add
                                           ).then_inc(l3_based[i], 1)

            pool.memset(ident[:], 0.0).then_inc(ones_set, 1)
            pool.memset(sel[:], 0.0).then_inc(ones_set, 1)
            pool.wait_ge(ones_set, 2)
            pool.affine_select(out=ident[:], in_=ident[:], compare_op=ALU.not_equal, fill=1.0, base=0,
                               pattern=[[-1, P]], channel_multiplier=1).then_inc(ident_set, 1)
            pool.memset(sel[:, ROWS - 1:ROWS], 1.0).then_inc(ones_set, 1)
            pool.memset(c_rows[:], 0.0).then_inc(ones_set, 1)
            pool.wait_ge(set_up, 1)
            prepare(0, 0)
            prepare(0, 1)

            def iteration(new, after, old, older):
                for s in range(SLOTS):
                    if is_graph(new, 1) and s == LATER_SET_UP_SLOT:
                        pool.wait_ge(later_weights_in, 16 * LATER_WEIGHTS)
                        pool.wait_ge(affine_set, 2)
                        pool.wait_ge(eps_set, 2)
                        pool.wait_ge(mask_set, 1)
                    g, place0 = tail_graph(s, old, older)
                    if s == 12 and new is not None:
                        coefficients(new, 0)
                    if s == 4 and old is not None:
                        coefficients(old, 1)
                    later_layers(g, place0, place0 + FINE // 2)
                    if s + 2 < SLOTS and new is not None:
                        prepare(new, s + 2)
                    if s + 1 == SLOTS and after is not None:
                        prepare(after, 0)
                        prepare(after, 1)
                    later_layers(g, place0 + FINE // 2, place0 + FINE)

            program(pool, iteration)


_INS = ['x', 'adj', 'nodemask', 'L0_gnn_W1', 'L0_gnn_b1', 'L0_gnn_W2', 'L0_gnn_b2', 'L0_gnn_gamma', 'L0_gnn_beta',
        'L1_gnn_W', 'L1_gnn_b', 'L2_gnn_W1', 'L2_gnn_b1', 'L2_gnn_W2', 'L2_gnn_b2', 'L2_gnn_eps',
        'L3_gnn_Ws', 'L3_gnn_bs', 'L3_gnn_gammas', 'L3_gnn_betas']


def kernel(**inputs):
    import numpy as np
    import concourse.bacc as bacc
    from concourse.bass_utils import run_bass_kernel_spmd

    nc = bacc.Bacc("TRN2", target_bir_lowering=False, num_devices=1)
    arrays, args = {}, []
    for name in _INS:
        a = np.ascontiguousarray(inputs[name])
        arrays[f"in_{name}_dram"] = a
        args.append(nc.dram_tensor(f"in_{name}_dram", a.shape, mybir.dt.from_np(a.dtype), kind="ExternalInput").ap())
    shape = tuple(inputs["x"].shape)
    args.append(nc.dram_tensor("out_dram", shape, F32, kind="ExternalOutput").ap())
    build(nc, *args)
    r = run_bass_kernel_spmd(nc, [arrays], core_ids=[0])
    return r.results[0]["out_dram"]
```
